# Optimizing a Trainium2 kernel written in Bass

```python
import numpy as np
import jax
import jax.numpy as jnp

def _softmax(x, axis=-1):
    return jax.nn.softmax(x, axis=axis)

def _gelu(x):
    return jax.nn.gelu(x, approximate=True)

def _silu(x):
    return jax.nn.silu(x)

def _sigmoid(x):
    return jax.nn.sigmoid(x)

def _layernorm(x, axis=-1, eps=1e-05):
    m = jnp.mean(x, axis=axis, keepdims=True)
    v = jnp.var(x, axis=axis, keepdims=True)
    return (x - m) / jnp.sqrt(v + eps)

def _scatter_add(tgt, idx, src, axis=0):
    return tgt.at[idx].add(src)

def _segment_sum(src, seg, n):
    return jax.ops.segment_sum(src, seg, n)
kernel_name = 'mk_gnn_ffn_d1_gnn_r8_880d69'

def setup_inputs(seed: int=0):
    np.random.seed(seed)
    _w = jnp.asarray

    def _rec_inputs():
        import jax
        import jax.numpy as jnp
        _gk = jax.random.key(seed)
        x = -0.0002117 + 1 * jax.random.normal(jax.random.fold_in(_gk, 1), (1250, 512), jnp.float32)
        src = jax.random.randint(jax.random.fold_in(_gk, 2), (20000,), 0, 1250, jnp.int32)
        dst = jnp.minimum((1250 * jax.random.uniform(jax.random.fold_in(_gk, 3), (20000,)) ** 2.0).astype(jnp.int32), 9999)
        _o = jnp.argsort(dst, stable=True)
        src = src[_o]
        dst = dst[_o]
        return (x, src, dst)
    x, src, dst = _rec_inputs()

    def _L0_gnn_setup():
        import jax, jax.numpy as jnp
        import numpy as np
        N_NODES = 6250

        def _gcn_conv(x, row, col, W, b, n_nodes):
            h = x @ W
            deg = jax.ops.segment_sum(jnp.ones(col.shape[0], x.dtype), col, num_segments=n_nodes)
            dis = jnp.where(deg > 0, jax.lax.rsqrt(deg), 0.0)
            norm = dis[row] * dis[col]
            msg = h[row] * norm[:, None]
            out = jax.ops.segment_sum(msg, col, num_segments=n_nodes)
            return out + b
        key = jax.random.key(seed)
        k1, k2, k3, k4 = jax.random.split(key, 4)
        N, E, FIN, FH = (N_NODES, 100000, 512, 512)
        x = jax.random.normal(k1, (N, FIN), dtype=jnp.float32)
        edge_index = jax.random.randint(k2, (2, E), 0, N, dtype=jnp.int64)
        W1 = jax.random.normal(k3, (FIN, FH), dtype=jnp.float32) * (1.0 / np.sqrt(FIN))
        b1 = jnp.zeros((FH,), jnp.float32)
        W2 = jax.random.normal(k4, (FH, FH), dtype=jnp.float32) * (1.0 / np.sqrt(FH))
        b2 = jnp.zeros((FH,), jnp.float32)
        return {'x': x, 'edge_index': edge_index, 'W1': W1, 'b1': b1, 'W2': W2, 'b2': b2}
    _L0_gnn_all = _L0_gnn_setup()
    _L0_gnn_in = {k: v for k, v in _L0_gnn_all.items() if k in ('W1', 'b1', 'W2', 'b2')}
    del _L0_gnn_all

    def _L0_ffn_setup():
        import jax, jax.numpy as jnp
        import numpy as np
        TOP_K = 2
        key = jax.random.key(seed)
        ks = jax.random.split(key, 4)
        b, t, d, e, h = (2, 256, 512, 8, 1024)
        scale = 0.02
        return {'x': jax.random.normal(ks[0], (b, t, d), dtype=jnp.float32), 'router_w': jax.random.normal(ks[1], (e, d), dtype=jnp.float32) * scale, 'router_b': jnp.zeros((e,), dtype=jnp.float32), 'fc1_w': jax.random.normal(ks[2], (e, 2 * h, d), dtype=jnp.float32) * scale, 'fc1_b': jnp.zeros((e, 2 * h), dtype=jnp.float32), 'fc2_w': jax.random.normal(ks[3], (e, d, h), dtype=jnp.float32) * scale, 'fc2_b': jnp.zeros((e, d), dtype=jnp.float32)}
    _L0_ffn_all = _L0_ffn_setup()
    _L0_ffn_in = {k: v for k, v in _L0_ffn_all.items() if k in ('router_w', 'router_b', 'fc1_w', 'fc1_b', 'fc2_w', 'fc2_b')}
    del _L0_ffn_all
    return {'x': x, 'src': src, 'dst': dst, 'L0_gnn_W1': _L0_gnn_in['W1'], 'L0_gnn_b1': _L0_gnn_in['b1'], 'L0_gnn_W2': _L0_gnn_in['W2'], 'L0_gnn_b2': _L0_gnn_in['b2'], 'L0_ffn_router_w': _L0_ffn_in['router_w'], 'L0_ffn_router_b': _L0_ffn_in['router_b'], 'L0_ffn_fc1_w': _L0_ffn_in['fc1_w'], 'L0_ffn_fc1_b': _L0_ffn_in['fc1_b'], 'L0_ffn_fc2_w': _L0_ffn_in['fc2_w'], 'L0_ffn_fc2_b': _L0_ffn_in['fc2_b']}

def reference(x, src, dst, L0_gnn_W1, L0_gnn_b1, L0_gnn_W2, L0_gnn_b2, L0_ffn_router_w, L0_ffn_router_b, L0_ffn_fc1_w, L0_ffn_fc1_b, L0_ffn_fc2_w, L0_ffn_fc2_b):
    import jax
    import jax.numpy as jnp

    def _L0_gnn_ref(x, edge_index, W1, b1, W2, b2):
        import jax, jax.numpy as jnp
        import numpy as np
        N_NODES = 6250

        def _gcn_conv(x, row, col, W, b, n_nodes):
            h = x @ W
            deg = jax.ops.segment_sum(jnp.ones(col.shape[0], x.dtype), col, num_segments=n_nodes)
            dis = jnp.where(deg > 0, jax.lax.rsqrt(deg), 0.0)
            norm = dis[row] * dis[col]
            msg = h[row] * norm[:, None]
            out = jax.ops.segment_sum(msg, col, num_segments=n_nodes)
            return out + b
        n = x.shape[0]
        loops = jnp.arange(n, dtype=edge_index.dtype)
        row = jnp.concatenate([edge_index[0], loops])
        col = jnp.concatenate([edge_index[1], loops])
        h = _gcn_conv(x, row, col, W1, b1, n)
        h = jax.nn.relu(h)
        return _gcn_conv(h, row, col, W2, b2, n)

    def _L0_ffn_ref(x, router_w, router_b, fc1_w, fc1_b, fc2_w, fc2_b):
        import jax, jax.numpy as jnp
        import numpy as np
        TOP_K = 2
        n_experts = router_w.shape[0]
        temp = 1.0
        logits = (jnp.einsum('btd,ed->bte', x, router_w) + router_b) / temp
        topk_val, topk_idx = jax.lax.top_k(logits, TOP_K)
        weights = jax.nn.softmax(topk_val, axis=-1)
        onehot = jax.nn.one_hot(topk_idx, n_experts, dtype=x.dtype)
        cw = jnp.einsum('btk,btke->bte', weights, onehot)
        h = jnp.einsum('btd,efd->btef', x, fc1_w) + fc1_b
        h1, h2 = jnp.split(h, 2, axis=-1)
        a = jax.nn.silu(h1) * h2
        y = jnp.einsum('bteh,edh->bted', a, fc2_w) + fc2_b
        out = jnp.einsum('bted,bte->btd', y, cw)
        return out
    edge_index = jnp.stack([src, dst])
    x = x + _L0_gnn_ref(_layernorm(x, axis=-1), edge_index, L0_gnn_W1, L0_gnn_b1, L0_gnn_W2, L0_gnn_b2)
    x = x + _L0_ffn_ref(_layernorm(x, axis=-1)[None], L0_ffn_router_w, L0_ffn_router_b, L0_ffn_fc1_w, L0_ffn_fc1_b, L0_ffn_fc2_w, L0_ffn_fc2_b)[0]
    return x

_drawn_inputs = setup_inputs


def setup_inputs(seed=0):
    import zlib

    import numpy as np

    out = dict(_drawn_inputs(seed))
    spreads = {'L0_gnn_b1': (0.0, 0.1),
     'L0_gnn_b2': (0.0, 0.1),
     'L0_ffn_router_b': (0.0, 0.1),
     'L0_ffn_fc1_b': (0.0, 0.512),
     'L0_ffn_fc2_b': (0.0, 0.1)}
    factors = {}
    for name, (base, spread) in spreads.items():
        noise = np.random.default_rng([zlib.crc32(name.encode()), seed]).standard_normal(out[name].shape)
        drawn = base * np.exp(spread * noise) if base else spread * noise
        out[name] = jnp.asarray(drawn.astype(out[name].dtype))
    for name, factor in factors.items():
        out[name] = (out[name] * factor).astype(out[name].dtype)
    return out
```

```python
from contextlib import ExitStack

import concourse.bass as bass
from concourse import mybir

F32 = mybir.dt.float32
F32R = mybir.dt.float32r
BF16 = mybir.dt.bfloat16
FP16 = mybir.dt.float16
I32 = mybir.dt.int32
ALU = mybir.AluOpType
ACT = mybir.ActivationFunctionType
AX = mybir.AxisListType

P = 128
N = 1250
D = 512
EDGES = 20000
NT = -(-N // P)
NP = NT * P
TAIL = N - (NT - 1) * P
ET = 2 * -(-EDGES // (2 * P))
EP = ET // 2
KD = D // P
EX = 8
TOP = 2
HID = 1024
CH = 6
ACT_CHUNKS = (1, 3, 2, 4, 5)
CW = KD * D
MAXT = (TOP * N + (P - 1) * EX + EX) // P
MINT = -(-TOP * N // P)
EPS = 1e-5
NO_NODE = 4095


def build(nc, x, src, dst, W1, b1, W2, b2, rw, rb, wall, fc1b, fc2b, out):
    rows_dram = nc.dram_tensor("expert_rows", (( MAXT + 1) * P, D), F32).ap()
    y_dram = nc.dram_tensor("expert_out", ((MAXT + 1) * P, D), F32).ap()

    with ExitStack() as ctx:
        def sb(name, shape, dt, c=ctx):
            return c.enter_context(nc.sbuf_tensor(name, shape, dt))

        def sem(name):
            return ctx.enter_context(nc.semaphore(name))

        ps = ctx.enter_context(nc.psum_tensor("ps", [P, 8, 512], F32))
        ident = sb("ident", [P, P], F32)
        xres = sb("xres", [P, NT, D], F32)
        raw = sb("raw", [P, CH, CW], F32)
        wts = sb("wts", [P, TOP, NT], F32)
        slots = sb("slots", [P, TOP, NT], I32)
        yslots = sb("yslots", [P, TOP, NT], I32)
        gstart = sb("gstart", [1, EX + 1], I32)

        raw_in = [sem(f"raw_in{c}") for c in range(CH)]
        router_done = sem("router_done")
        scattered = sem("scattered")
        graph_block(nc, ctx, locals())
        expert_block(nc, ctx, locals())


def graph_block(nc, outer, env):
    x, src, dst, W1, b1, W2, b2, rw, rb, wall, fc2b = (env[k] for k in (
        "x", "src", "dst", "W1", "b1", "W2", "b2", "rw", "rb", "wall", "fc2b"))
    ident, xres, raw, wts, slots, yslots, gstart, ps = (env[k] for k in (
        "ident", "xres", "raw", "wts", "slots", "yslots", "gstart", "ps"))
    raw_in, scattered, rows_dram, y_dram = env["raw_in"], env["scattered"], env["rows_dram"], env["y_dram"]

    with ExitStack() as ctx:
        def sb(name, shape, dt):
            return ctx.enter_context(nc.sbuf_tensor(name, shape, dt))

        def sem(name):
            return ctx.enter_context(nc.semaphore(name))

        CT = sb("CT", [P, NT, NP], F32)
        h = sb("h", [P, NT, D], F32)
        h1T = sb("h1T", [P, KD, NP], F32)
        xn1 = h1T[:, :, :].rearrange("p a b -> p (a b)").rearrange("p (t d) -> p t d", t=NT)
        flags = h1T[:, :, :].rearrange("p a b -> p (a b)")[:, 0:NT * ET // 2].bitcast(BF16)
        spare = h1T[:, :, :].rearrange("p a b -> p (a b)")[:, NT * ET // 2:]
        Wg = sb("Wg", [P, KD, D], F32)
        Cs = sb("Cs", [P, NP], F32)
        hot_s = sb("hot_s", [P, 2, NP + 4], BF16)
        hot_d = sb("hot_d", [P, 2, P], BF16)
        eyez = sb("eyez", [P, 2 * NP], BF16)
        iota = sb("iota", [P, NP], FP16)
        xn = sb("xn", [P, 2, D], F32)
        xnT = sb("xnT", [P, 2, KD, P], F32)
        dis_bc = sb("dis_bc", [P, NP], F32)
        b2_bc = sb("b2_bc", [P, D], F32)
        src_i = sb("src_i", [P, ET], I32)
        dst_i = sb("dst_i", [P, ET], I32)
        src_f = sb("src_f", [P, ET], F32)
        dst_f = sb("dst_f", [P, ET], F32)
        b1c = sb("b1c", [P, KD], F32)
        rwT = sb("rwT", [P, KD, EX], F32)
        rb_bc = sb("rb_bc", [P, EX], F32)
        stat = sb("stat", [P, 6], F32)
        mv = sb("mv", [P, NT, 2], F32)
        sd = sb("sd", [P, NT], F32)
        rs = sb("rs", [P, NT], F32)
        deg = sb("deg", [P, NT], F32)
        dis = sb("dis", [P, NT], F32)
        t4 = sb("t4", [P, 4, NT], F32)
        ones_b = sb("ones_b", [P, P], BF16)
        ones_f = sb("ones_f", [P, P], F32)
        below = sb("below", [P, P], BF16)
        lg = sb("lg", [P, NT, EX], F32)
        valid = sb("valid", [P, NT], F32)
        iota_e = sb("iota_e", [P, NT, EX], F32)
        sc8 = sb("sc8", [P, 2, NT, EX], F32)
        top = sb("top", [P, TOP, NT, EX], F32)
        mx = sb("mx", [P, 6, NT], F32)
        mem_b = sb("mem_b", [P, NT, EX], BF16)
        rank = sb("rank", [P, NT, EX], F32)
        e8 = sb("e8", [P, 6, EX], F32)
        thr = sb("thr", [P, EX, NT], F32)
        cmp8 = sb("cmp8", [P, EX, NT], F32)
        rng_i = sb("rng_i", [1, 2, NT], I32)
        cwT = Cs[0:EX, :].rearrange("p (t n) -> p t n", t=NT)
        fc2b_sb = dis_bc[0:EX, 0:D]

        edges_in = sem("edges_in")
        x_in = [sem(f"x_in{i}") for i in range(4)]
        w1_in = sem("w1_in")
        w2_in = sem("w2_in")
        consts_in = sem("consts_in")
        fc2b_in = sem("fc2b_in")
        zero_out = sem("zero_out")
        pool_made = sem("pool_made")
        flags_made = sem("flags_made")
        flags_summed = sem("flags_summed")
        ranges_made = sem("ranges_made")
        dve = sem("dve")
        var_made = sem("var_made")
        root_made = sem("root_made")
        xn_made = sem("xn_made")
        xnT_ps = sem("xnT_ps")
        xnT_made = sem("xnT_made")
        h_ps = sem("h_ps")
        h_made = sem("h_made")
        hot_made = sem("hot_made")
        hot_free = sem("hot_free")
        counts_ps = sem("counts_ps")
        counts_out = sem("counts_out")
        ct_ps = sem("ct_ps")
        ct_made = sem("ct_made")
        diag_made = sem("diag_made")
        disbc_ps = sem("disbc_ps")
        disbc_made = sem("disbc_made")
        h_scaled = sem("h_scaled")
        agg1_ps = sem("agg1_ps")
        agg1_scaled = sem("agg1_scaled")
        h1T_made = sem("h1T_made")
        agg2_ps = sem("agg2_ps")
        agg2_out = sem("agg2_out")
        lg_ps = sem("lg_ps")
        mem_made = sem("mem_made")
        rank_ps = sem("rank_ps")
        slots_made = sem("slots_made")
        cw_made = sem("cw_made")
        cwT_ps = sem("cwT_ps")
        cwT_made = sem("cwT_made")
        eb_ps = sem("eb_ps")

        GROUPS = [(0, 512), (512, 1024), (1024, NP)]
        bank = lambda i: ps[:, i, :]
        flat = ps[:, :, :].rearrange("p b n -> p (b n)")

        block = ctx.enter_context(nc.Block())

        @block.sync
        def _(sp):
            sp.dma_start(dst_i[:, :], dst).then_inc(edges_in, 16)
            sp.dma_start(src_i[:, :], src).then_inc(edges_in, 16)
            xt = x[0:(NT - 1) * P, :].rearrange("(t p) d -> p t d", p=P)
            for i in range(3):
                sp.dma_start(xres[:, 3 * i:3 * i + 3, :], xt[:, 3 * i:3 * i + 3, :]).then_inc(x_in[i], 16)
            sp.dma_start(Wg[:, :, :], W1.rearrange("(k p) n -> p k n", p=P)).then_inc(w1_in, 16)
            sp.wait_ge(pool_made, 1)
            sp.dma_start(xres[0:TAIL, NT - 1, :], x[(NT - 1) * P:N, :]).then_inc(x_in[3], 16)
            sp.dma_start(b1c[:, :], b1).then_inc(consts_in, 16)
            sp.dma_start(rwT[:, :, :], rw.rearrange("(k p) e -> p k e", p=P)).then_inc(consts_in, 16)
            sp.dma_start(rb_bc[:, :], rb.partition_broadcast(P)).then_inc(consts_in, 16)
            sp.dma_start(b2_bc[:, :], b2.partition_broadcast(P)).then_inc(consts_in, 16)
            for c in range(CH):
                sp.dma_start(raw[:, c, :], wall[c, :, :]).then_inc(raw_in[c], 16)
            sp.wait_ge(pool_made, 3)
            zeros = eyez[:, 0:2 * D].bitcast(F32)
            for g in range(MAXT + 1):
                sp.dma_start(rows_dram[g * P:(g + 1) * P, :], zeros).then_inc(zero_out, 16)
            for g in range(MINT + 1, MAXT + 1):
                sp.dma_start(y_dram[g * P:(g + 1) * P, :], zeros).then_inc(zero_out, 16)
            sp.wait_ge(h_ps, NT)
            sp.dma_start(Wg[:, :, :], W2.rearrange("(k p) n -> p k n", p=P)).then_inc(w2_in, 16)
            sp.wait_ge(agg1_scaled, 3 * KD)
            sp.dma_start(fc2b_sb, fc2b).then_inc(fc2b_in, 16)

        @block.gpsimd
        def _(pool):
            made = 0

            def step(ins):
                nonlocal made
                made += 1
                ins.then_inc(pool_made, 1)
                pool.wait_ge(pool_made, made)

            step(pool.memset(xres[:, NT - 1, :], 0.0))
            step(pool.memset(eyez[:, :], 0.0))
            mid = eyez[:, NP - P:NP]
            step(pool.affine_select(out=mid, in_=mid, compare_op=ALU.not_equal, fill=1.0, base=0,
                                    pattern=[[-1, P]], channel_multiplier=1))
            step(pool.memset(ident[:, :], 0.0))
            step(pool.affine_select(out=ident[:, :], in_=ident[:, :], compare_op=ALU.not_equal, fill=1.0,
                                    base=0, pattern=[[-1, P]], channel_multiplier=1))
            step(pool.memset(ones_b[:, :], 1.0))
            step(pool.iota(iota[:, :], pattern=[[1, NP]], base=0, channel_multiplier=0,
                           allow_small_or_imprecise_dtypes=True))
            step(pool.memset(hot_s[:, :, :], 1.0))
            step(pool.iota(spare[0:1, 0:ET], pattern=[[1, EP], [0, 2]], base=1, channel_multiplier=0,
                           allow_small_or_imprecise_dtypes=True))
            step(pool.iota(spare[0:1, ET:2 * ET], pattern=[[-1, EP], [0, 2]], base=EP, channel_multiplier=0,
                           allow_small_or_imprecise_dtypes=True))
            step(pool.memset(ones_f[:, :], 1.0))
            step(pool.affine_select(out=below[:, :], in_=ones_b[:, :], compare_op=ALU.is_gt, fill=0.0,
                                    base=0, pattern=[[1, P]], channel_multiplier=-1))
            step(pool.memset(valid[:, :], 1.0))
            step(pool.affine_select(out=valid[:, :], in_=valid[:, :], compare_op=ALU.is_gt, fill=0.0,
                                    base=N, pattern=[[-P, NT]], channel_multiplier=-1))
            step(pool.iota(iota_e[:, :, :], pattern=[[0, NT], [1, EX]], base=-EX, channel_multiplier=0,
                           allow_small_or_imprecise_dtypes=True))
            step(pool.iota(thr[:, :, :], pattern=[[0, EX], [P, NT]], base=0, channel_multiplier=0,
                           allow_small_or_imprecise_dtypes=True))
            pool.wait_ge(zero_out, 16 * (2 * MAXT + 1 - MINT))
            pool.wait_ge(slots_made, 1)
            for t in range(NT):
                n = P if t < NT - 1 else TAIL
                for k in range(TOP):
                    pool.indirect_dma_start(
                        rows_dram, bass.IndirectOffsetOnAxis(slots[0:n, k, t:t + 1], 0),
                        xn1[0:n, t, :], None).then_inc(scattered, 16)
            pool.wait_ge(scattered, 16 * NT * TOP)

        @block.tensor
        def _(pe):
            pe.wait_ge(flags_made, 1)
            pe.wait_ge(pool_made, 6)
            for a in range(0, NT * ET, 512):
                b = min(a + 512, NT * ET)
                mm = pe.matmul(flat[0:1, a:b], ones_b[:, 0:1], flags[:, a:b], start=True, stop=True)
            mm.then_inc(flags_summed, 1)

            def transposes(t, of, to):
                for k in range(KD):
                    tr = pe.transpose(to[:, k * P:(k + 1) * P], of[:, k * P:(k + 1) * P], ident[:, :])
                return tr

            for t in range(NT + 1):
                if t < NT:
                    pe.wait_ge(xn_made, t + 1)
                    if t >= 2:
                        pe.wait_ge(xnT_made, t - 1)
                    transposes(t, xn[:, t % 2, :], bank(6 + t % 2)).then_inc(xnT_ps, 1)
                if t >= 1:
                    s = t - 1
                    if s == 0:
                        pe.wait_ge(w1_in, 16)
                    pe.wait_ge(xnT_made, s + 1)
                    if s >= 2:
                        pe.wait_ge(h_made, s - 1)
                    for k in range(KD):
                        mm = pe.matmul(bank(4 + s % 2), xnT[:, s % 2, k, :], Wg[:, k, :],
                                       start=(k == 0), stop=(k == KD - 1))
                    mm.then_inc(h_ps, 1)

            n_hot = pe.alloc_register("pe_hot")
            pe.reg_mov(n_hot, 0)
            pe.wait_ge(ranges_made, 1)
            pe.wait_ge(pool_made, 8)
            pe.sem_inc(hot_free, 2)

            def ct_block(b):
                pe.wait_ge(counts_out, b + 1)
                for q in range(3):
                    n = 3 * b + q
                    if n >= 2:
                        pe.wait_ge(ct_made, n - 1)
                    for k in range(4 * q, min(4 * q + 4, NT)):
                        tr = pe.transpose(bank(6 + n % 2)[:, (k % 4) * P:(k % 4 + 1) * P],
                                          Cs[:, k * P:(k + 1) * P], ident[:, :])
                    tr.then_inc(ct_ps, 1)

            for b in range(NT):
                o = flat[:, 1536 * (b % 2):1536 * (b % 2) + NP + 1]
                if b == 1:
                    pe.wait_ge(h_made, NT)
                if b >= 2:
                    pe.wait_ge(counts_out, b - 1)
                at = NP - P - b * P
                for lo, hi in ((0, 512), (512, 1024), (1024, NP + 1)):
                    pe.matmul(o[:, lo:hi], eyez[:, NP - P:NP], eyez[:, at + lo:at + hi],
                              start=True, stop=False, skip_group_check=True)
                first = pe.value_load(rng_i[0:1, 0, b:b + 1], min_val=0, max_val=EP - 1)
                last = pe.value_load(rng_i[0:1, 1, b:b + 1], min_val=1, max_val=EP)
                with pe.Fori(first, last):
                    for j in range(2):
                        pe.reg_add(n_hot, n_hot, 1)
                        pe.wait_ge(hot_made, n_hot)
                        for lo, hi in ((0, 512), (512, 1024), (1024, NP + 1)):
                            mm = pe.matmul(o[:, lo:hi], hot_d[:, j, :], hot_s[:, j, lo:hi],
                                           start=False, stop=False, skip_group_check=True)
                        mm.then_inc(hot_free, 1)
                pe.matmul(o[:, 0:1], eyez[:, NP - P:NP], eyez[:, 0:1], start=False, stop=True,
                          skip_group_check=True).then_inc(counts_ps, 1)
                if b >= 1:
                    ct_block(b - 1)
            ct_block(NT - 1)

            pe.wait_ge(pool_made, 11)
            for t in range(NT):
                pe.wait_ge(diag_made, t + 1)
                mm = pe.matmul(flat[:, t * P:(t + 1) * P], ones_f[:, :], xn[:, t % 2, 0:P],
                               start=(t % 4 == 0), stop=True, skip_group_check=True)
                mm.then_inc(disbc_ps, 1)

            n = 0
            pe.wait_ge(h_scaled, NT)
            pe.wait_ge(ct_made, 3 * NT)
            for lo, hi in GROUPS:
                for j in range(KD):
                    if n >= 2:
                        pe.wait_ge(agg1_scaled, n - 1)
                    for k in range(NT):
                        mm = pe.matmul(bank(3 + n % 2)[:, 0:hi - lo], h[:, k, j * P:(j + 1) * P],
                                       CT[:, k, lo:hi], start=(k == 0), stop=(k == NT - 1))
                    mm.then_inc(agg1_ps, 1)
                    n += 1
            pe.wait_ge(w2_in, 16)
            for m in range(NT):
                pe.wait_ge(h1T_made, KD * (m // 4 + 1))
                if m >= 2:
                    pe.wait_ge(h_made, NT + m - 1)
                for k in range(KD):
                    mm = pe.matmul(bank(5 + m % 2), h1T[:, k, m * P:(m + 1) * P], Wg[:, k, :],
                                   start=(k == 0), stop=(k == KD - 1))
                mm.then_inc(h_ps, 1)
            pe.wait_ge(h_made, 2 * NT)
            pe.wait_ge(disbc_made, 1)
            for m in range(NT + 3):
                if m < NT:
                    if m >= 2:
                        pe.wait_ge(agg2_out, m - 1)
                    for k in range(NT):
                        mm = pe.matmul(bank(3 + m % 2), CT[:, k, m * P:(m + 1) * P], h[:, k, :],
                                       start=(k == 0), stop=(k == NT - 1))
                    mm.then_inc(agg2_ps, 1)
                if 1 <= m <= NT:
                    s = m - 1
                    pe.wait_ge(xn_made, NT + s + 1)
                    transposes(s, xn1[:, s, :], bank(6 + s % 2)).then_inc(xnT_ps, 1)
                if 2 <= m <= NT + 1:
                    s = m - 2
                    pe.wait_ge(xnT_made, NT + s + 1)
                    for k in range(KD):
                        mm = pe.matmul(bank(1)[:, s * EX:(s + 1) * EX], xnT[:, s % 2, k, :], rwT[:, k, :],
                                       start=(k == 0 and s == 0), stop=(k == KD - 1), skip_group_check=True)
                    mm.then_inc(lg_ps, 1)

            pe.wait_ge(mem_made, 1)
            mem = mem_b[:, :, :].rearrange("p t e -> p (t e)")
            pe.matmul(bank(2)[:, 0:NT * EX], below[:, :], mem, start=True, stop=False, skip_group_check=True)
            for s in range(1, NT):
                mm = pe.matmul(bank(2)[:, s * EX:NT * EX], ones_b[:, :], mem[:, 0:(NT - s) * EX],
                               start=False, stop=(s == NT - 1), skip_group_check=True)
            for t in range(NT):
                mm = pe.matmul(bank(5)[:, 0:EX], ones_b[:, :], mem_b[:, t, :], start=(t == 0),
                               stop=(t == NT - 1))
            mm.then_inc(rank_ps, 1)
            pe.wait_ge(fc2b_in, 16)
            for t in range(NT):
                pe.wait_ge(cw_made, 1)
                if t >= 2:
                    pe.wait_ge(cwT_made, t - 1)
                pe.transpose(bank(6 + t % 2)[0:EX, 0:P], sc8[:, 0, t, :], ident[:, :]).then_inc(cwT_ps, 1)
                pe.wait_ge(cwT_made, t + 1)
                if t >= 2:
                    pe.wait_ge(agg2_out, NT + t - 1)
                pe.matmul(bank(3 + t % 2), cwT[:, t, :], fc2b_sb, start=True, stop=True).then_inc(eb_ps, 1)

        @block.scalar
        def _(act):
            def root(n, to, of):
                act.wait_ge(var_made, n)
                act.activation(to, of, ACT.Sqrt).then_inc(root_made, 1)

            root(1, sd[:, 0:3], mv[:, 0:3, 1])
            for t in range(NT + 1):
                if t in (1, 4, 7):
                    g = (t + 2) // 3
                    root(g + 1, sd[:, 3 * g:min(3 * g + 3, NT)], mv[:, 3 * g:min(3 * g + 3, NT), 1])
                if t < NT:
                    act.wait_ge(xnT_ps, t + 1)
                    if t >= 2:
                        act.wait_ge(h_ps, t - 1)
                    act.activation(xnT[:, t % 2, :, :].rearrange("p k n -> p (k n)"), bank(6 + t % 2),
                                   ACT.Copy).then_inc(xnT_made, 1)
                if t >= 1:
                    act.wait_ge(h_ps, t)
                    act.activation(h[:, t - 1, :], bank(4 + (t - 1) % 2), ACT.Copy).then_inc(h_made, 1)

            def ct_block(b):
                for q in range(3):
                    n = 3 * b + q
                    m = min(4, NT - 4 * q)
                    act.wait_ge(ct_ps, n + 1)
                    act.activation(CT[:, 4 * q:4 * q + m, b * P:(b + 1) * P],
                                   bank(6 + n % 2)[:, 0:m * P].rearrange("p (k n) -> p k n", k=m),
                                   ACT.Copy).then_inc(ct_made, 1)

            for b in range(NT):
                act.wait_ge(counts_ps, b + 1)
                if b >= 1:
                    ct_needed = 3 * b
                    act.wait_ge(ct_ps, ct_needed)
                act.activation(deg[:, b:b + 1], flat[:, 1536 * (b % 2) + NP:1536 * (b % 2) + NP + 1], ACT.Copy)
                act.activation(Cs[:, :], flat[:, 1536 * (b % 2):1536 * (b % 2) + NP], ACT.Copy)\
                   .then_inc(counts_out, 1)
                ct_block(b)

            root(5, sd[:, :], t4[:, 3, :])
            act.wait_ge(disbc_ps, NT)
            act.activation(dis_bc[:, :], flat[:, 0:NP], ACT.Copy).then_inc(disbc_made, 1)
            act.wait_ge(consts_in, 64)
            n = 0
            for lo, hi in GROUPS:
                for j in range(KD):
                    act.wait_ge(agg1_scaled, n + 1)
                    act.activation(h1T[:, j, lo:hi], h1T[:, j, lo:hi], ACT.Relu, bias=b1c[:, j:j + 1])\
                       .then_inc(h1T_made, 1)
                    n += 1
            for m in range(NT):
                act.wait_ge(h_ps, NT + m + 1)
                if m == 0:
                    act.wait_ge(agg1_ps, 12)
                act.activation(h[:, m, :], bank(5 + m % 2), ACT.Copy, scale=dis[:, m:m + 1]).then_inc(h_made, 1)
            for m in range(NT):
                root(6 + m, sd[:, m:m + 1], mv[:, m, 1:2])
                act.wait_ge(xnT_ps, NT + m + 1)
                if m >= 2:
                    act.wait_ge(lg_ps, m - 1)
                act.activation(xnT[:, m % 2, :, :].rearrange("p k n -> p (k n)"), bank(6 + m % 2),
                               ACT.Copy).then_inc(xnT_made, 1)
            act.wait_ge(var_made, 6 + NT)
            act.activation(mx[:, 3, :], mx[:, 2, :], ACT.Exp).then_inc(root_made, 1)
            for t in range(NT):
                act.wait_ge(cwT_ps, t + 1)
                act.activation(cwT[:, t, :], bank(6 + t % 2)[0:EX, 0:P], ACT.Copy).then_inc(cwT_made, 1)

        @block.vector
        def _(v):
            done = 0

            def link(ins):
                nonlocal done
                done += 1
                ins.then_inc(dve, 1)
                v.wait_ge(dve, done)

            v.wait_ge(edges_in, 32)
            link(v.tensor_scalar(src_f[:, :], src_i[:, :], 0.0, None, ALU.add))
            link(v.tensor_scalar(dst_f[:, :], dst_i[:, :], 0.0, None, ALU.add))
            link(v.tensor_scalar(dst_i[:, :], dst_i[:, :], 7, None, ALU.arith_shift_right))
            for b in range(NT):
                f = v.tensor_scalar(flags[:, b * ET:(b + 1) * ET], dst_i[:, :], float(b), None, ALU.is_equal)
            f.then_inc(flags_made, 1)

            def rsqrt(y, s, var, a, b):
                link(v.reciprocal(y, s))
                link(v.tensor_tensor(a, y, y, ALU.mult))
                link(v.tensor_tensor(b, a, var, ALU.mult))
                link(v.tensor_scalar(a, b, -0.5, 1.5, ALU.mult, ALU.add))
                link(v.tensor_tensor(y, y, a, ALU.mult))

            def stats(t):
                link(v.bn_stats(stat[:, :], xres[:, t, :]))
                link(v.bn_aggr(mv[:, t, :], stat[:, :]))

            for g in range(4):
                a, b = 3 * g, min(3 * g + 3, NT)
                v.wait_ge(x_in[g], 16)
                if g == 3:
                    v.wait_ge(pool_made, 1)
                for t in range(a, b):
                    stats(t)
                v.tensor_scalar(mv[:, a:b, 1], mv[:, a:b, 1], EPS, None, ALU.add).then_inc(var_made, 1)
                v.wait_ge(root_made, g + 1)
                rsqrt(rs[:, a:b], sd[:, a:b], mv[:, a:b, 1], t4[:, 0, a:b], t4[:, 1, a:b])
                for t in range(a, b):
                    if t >= 2:
                        v.wait_ge(xnT_ps, t - 1)
                    v.tensor_scalar(xn[:, t % 2, :], xres[:, t, :], mv[:, t, 0:1], rs[:, t:t + 1],
                                    ALU.subtract, ALU.mult).then_inc(xn_made, 1)
                if g == 0:
                    v.wait_ge(flags_summed, 1)
                    v.wait_ge(pool_made, 10)
                    r = spare[0:1, 2 * ET:2 * ET + NT * ET]
                    r3 = r.rearrange("p (b t) -> p b t", b=NT)
                    link(v.tensor_scalar(r, flat[0:1, 0:NT * ET], 1.0, None, ALU.min))
                    r2 = spare[0:1, 2 * ET + NT * ET:2 * ET + 2 * NT * ET]
                    r23 = r2.rearrange("p (b t) -> p b t", b=NT)
                    lim = spare[0:1, 2 * ET + 2 * NT * ET:2 * ET + 2 * NT * ET + 4 * NT]
                    up = spare[0:1, 0:ET].unsqueeze(1).to_broadcast([1, NT, ET])
                    down = spare[0:1, ET:2 * ET].unsqueeze(1).to_broadcast([1, NT, ET])
                    link(v.tensor_tensor(r23, r3, up, ALU.mult))
                    link(v.tensor_reduce(lim[:, 0:NT], r23, AX.X, ALU.max))
                    link(v.tensor_tensor(r23, r3, down, ALU.mult))
                    link(v.tensor_reduce(lim[:, NT:2 * NT], r23, AX.X, ALU.max))
                    link(v.tensor_scalar(lim[:, 0:NT], lim[:, 0:NT], 1.0, None, ALU.max))
                    link(v.tensor_scalar(lim[:, NT:2 * NT], lim[:, NT:2 * NT], -1.0, float(EP), ALU.mult, ALU.add))
                    link(v.tensor_scalar(lim[:, 2 * NT:3 * NT], lim[:, 0:NT], -1.0, None, ALU.add))
                    link(v.tensor_tensor(rng_i[0:1, 0, :], lim[:, NT:2 * NT], lim[:, 2 * NT:3 * NT], ALU.min))
                    v.tensor_scalar(rng_i[0:1, 1, :], lim[:, 0:NT], 0.0, None, ALU.add).then_inc(ranges_made, 1)
                    v.wait_ge(ranges_made, 1)

            v.wait_ge(pool_made, 8)
            n_hot = v.alloc_register("v_hot")
            v.reg_mov(n_hot, 0)
            for b in range(NT):
                first = v.value_load(rng_i[0:1, 0, b:b + 1], min_val=0, max_val=EP - 1)
                last = v.value_load(rng_i[0:1, 1, b:b + 1], min_val=1, max_val=EP)
                with v.Fori(first, last) as i:
                    for j in range(2):
                        v.reg_add(n_hot, n_hot, 1)
                        v.wait_ge(hot_free, n_hot)
                        v.tensor_scalar(hot_s[:, j, 0:NP], iota[:, :], src_f[:, bass.ds(2 * i + j, 1)], None,
                                        ALU.is_equal)
                        v.tensor_scalar(hot_d[:, j, :], iota[:, b * P:(b + 1) * P],
                                        dst_f[:, bass.ds(2 * i + j, 1)], None, ALU.is_equal).then_inc(hot_made, 1)

            v.wait_ge(counts_out, NT)
            v.tensor_scalar(t4[:, 3, :], deg[:, :], 1.0, None, ALU.add).then_inc(var_made, 1)
            v.wait_ge(var_made, 5)
            v.wait_ge(root_made, 5)
            rsqrt(dis[:, :], sd[:, :], t4[:, 3, :], t4[:, 0, :], t4[:, 1, :])
            for t in range(NT):
                if t >= 2:
                    v.wait_ge(disbc_ps, t - 1)
                v.tensor_scalar(xn[:, t % 2, 0:P], ident[:, :], dis[:, t:t + 1], None, ALU.mult)\
                 .then_inc(diag_made, 1)
            v.wait_ge(h_made, NT)
            for t in range(NT):
                v.tensor_scalar(h[:, t, :], h[:, t, :], dis[:, t:t + 1], None, ALU.mult).then_inc(h_scaled, 1)
            v.wait_ge(disbc_made, 1)
            n = 0
            for lo, hi in GROUPS:
                for j in range(KD):
                    v.wait_ge(agg1_ps, n + 1)
                    v.tensor_tensor(h1T[:, j, lo:hi], bank(3 + n % 2)[:, 0:hi - lo], dis_bc[:, lo:hi], ALU.mult)\
                     .then_inc(agg1_scaled, 1)
                    n += 1
            v.wait_ge(consts_in, 64)
            for t in range(NT):
                f = v.tensor_tensor(xres[:, t, :], xres[:, t, :], b2_bc[:, :], ALU.add)
            link(f)
            v.wait_ge(h_ps, 2 * NT)
            for m in range(NT):
                v.wait_ge(agg2_ps, m + 1)
                f = v.scalar_tensor_tensor(xres[:, m, :], bank(3 + m % 2), dis[:, m:m + 1], xres[:, m, :],
                                           ALU.mult, ALU.add)
                f.then_inc(agg2_out, 1)
                v.wait_ge(agg2_out, m + 1)
                stats(m)
                v.tensor_scalar(mv[:, m, 1:2], mv[:, m, 1:2], EPS, None, ALU.add).then_inc(var_made, 1)
                v.wait_ge(var_made, 6 + m)
                v.wait_ge(root_made, 6 + m)
                rsqrt(rs[:, m:m + 1], sd[:, m:m + 1], mv[:, m, 1:2], t4[:, 0, m:m + 1], t4[:, 1, m:m + 1])
                v.tensor_scalar(xn1[:, m, :], xres[:, m, :], mv[:, m, 0:1], rs[:, m:m + 1],
                                ALU.subtract, ALU.mult).then_inc(xn_made, 1)

            v.wait_ge(lg_ps, NT)
            v.wait_ge(pool_made, 16)
            bc = lambda a: a.unsqueeze(2).to_broadcast([P, NT, EX])
            link(v.tensor_tensor(lg[:, :, :], bank(1)[:, 0:NT * EX].rearrange("p (t e) -> p t e", t=NT),
                                 rb_bc[:, :].unsqueeze(1).to_broadcast([P, NT, EX]), ALU.add))
            for k in range(TOP):
                link(v.tensor_reduce(mx[:, k, :], lg[:, :, :], AX.X, ALU.max))
                link(v.tensor_tensor(sc8[:, 0, :, :], lg[:, :, :], bc(mx[:, k, :]), ALU.is_equal))
                link(v.tensor_tensor(sc8[:, 1, :, :], sc8[:, 0, :, :], iota_e[:, :, :], ALU.mult))
                link(v.tensor_reduce(mx[:, 4, :], sc8[:, 1, :, :], AX.X, ALU.min))
                link(v.tensor_tensor(top[:, k, :, :], iota_e[:, :, :], bc(mx[:, 4, :]), ALU.is_equal))
                if k == 0:
                    link(v.scalar_tensor_tensor(lg[:, :, :], top[:, 0, :, :], -3.0e38, lg[:, :, :],
                                                ALU.mult, ALU.add))
            v.tensor_tensor(mx[:, 2, :], mx[:, 1, :], mx[:, 0, :], ALU.subtract).then_inc(var_made, 1)
            link(v.tensor_tensor(sc8[:, 0, :, :], top[:, 0, :, :], top[:, 1, :, :], ALU.add))
            v.tensor_tensor(mem_b[:, :, :], sc8[:, 0, :, :], bc(valid[:, :]), ALU.mult).then_inc(mem_made, 1)
            v.wait_ge(var_made, 6 + NT)
            v.wait_ge(root_made, 6 + NT)
            link(v.tensor_scalar(mx[:, 4, :], mx[:, 3, :], 1.0, None, ALU.add))
            link(v.reciprocal(wts[:, 0, :], mx[:, 4, :]))
            link(v.tensor_tensor(wts[:, 1, :], wts[:, 0, :], mx[:, 3, :], ALU.mult))
            v.wait_ge(rank_ps, 1)
            link(v.tensor_scalar(e8[:, 0, :], bank(5)[:, 0:EX], 1.0, None, ALU.max))
            link(v.tensor_tensor(cmp8[:, :, :], e8[:, 0, :].unsqueeze(2).to_broadcast([P, EX, NT]),
                                 thr[:, :, :], ALU.is_gt))
            link(v.tensor_reduce(e8[:, 1, :], cmp8[:, :, :], AX.X, ALU.add))
            a, b = 1, 2
            for s in (1, 2, 4):
                v.tensor_scalar(e8[:, b, 0:s], e8[:, a, 0:s], 0.0, None, ALU.add)
                link(v.tensor_tensor(e8[:, b, s:EX], e8[:, a, s:EX], e8[:, a, 0:EX - s], ALU.add))
                a, b = b, b + 1
            link(v.tensor_tensor(e8[:, 5, :], e8[:, 4, :], e8[:, 1, :], ALU.subtract))
            v.tensor_scalar(gstart[0:1, 0:EX], e8[0:1, 5, :], 0.0, None, ALU.add)
            v.tensor_scalar(gstart[0:1, EX:EX + 1], e8[0:1, 4, EX - 1:EX], 0.0, None, ALU.add)
            link(v.tensor_scalar(e8[:, 2, :], e8[:, 5, :], float(P), None, ALU.mult))
            link(v.tensor_tensor(rank[:, :, :], bank(2)[:, 0:NT * EX].rearrange("p (t e) -> p t e", t=NT),
                                 e8[:, 2, :].unsqueeze(1).to_broadcast([P, NT, EX]), ALU.add))
            for k in range(TOP):
                link(v.tensor_tensor(sc8[:, 0, :, :], top[:, k, :, :], rank[:, :, :], ALU.mult))
                link(v.tensor_reduce(mx[:, 4, :], sc8[:, 0, :, :], AX.X, ALU.add))
                link(v.tensor_scalar(slots[:, k, :], mx[:, 4, :], 0.0, None, ALU.add))
                link(v.tensor_scalar(yslots[:, k, :], mx[:, 4, :], float(P), None, ALU.add))
            v.sem_inc(slots_made, 1)
            link(v.tensor_tensor(sc8[:, 0, :, :], top[:, 0, :, :], bc(wts[:, 0, :]), ALU.mult))
            link(v.tensor_tensor(sc8[:, 1, :, :], top[:, 1, :, :], bc(wts[:, 1, :]), ALU.mult))
            v.tensor_tensor(sc8[:, 0, :, :], sc8[:, 0, :, :], sc8[:, 1, :, :], ALU.add).then_inc(cw_made, 1)
            for t in range(NT):
                v.wait_ge(eb_ps, t + 1)
                v.tensor_tensor(xres[:, t, :], xres[:, t, :], bank(3 + t % 2), ALU.add).then_inc(agg2_out, 1)


def expert_block(nc, outer, env):
    wall, fc1b, out = env["wall"], env["fc1b"], env["out"]
    ident, xres, raw, wts, yslots, gstart, ps = (env[k] for k in (
        "ident", "xres", "raw", "wts", "yslots", "gstart", "ps"))
    raw_in, rows_dram, y_dram = env["raw_in"], env["rows_dram"], env["y_dram"]

    with ExitStack() as ctx:
        def sb(name, shape, dt):
            return ctx.enter_context(nc.sbuf_tensor(name, shape, dt))

        def sem(name):
            return ctx.enter_context(nc.semaphore(name))

        whi = sb("whi", [P, CH, KD, D], F32R)
        wlo = sb("wlo", [P, CH, KD, D], F32R)
        bias = sb("bias", [P, 2, 2, D], F32)
        xg = sb("xg", [P, D], F32)
        xhi = sb("xhi", [P, KD, P], F32R)
        xlo = sb("xlo", [P, KD, P], F32R)
        t1 = sb("t1", [P, 2, D], F32)
        sl = sb("sl", [P, 2, D], F32)
        a = sb("a", [P, 2, D], F32)
        ahi = sb("ahi", [P, 2, KD, P], F32R)
        alo = sb("alo", [P, 2, KD, P], F32R)
        ysb = sb("ysb", [P, D], F32)

        bias_in = sem("bias_in")
        bias_free = sem("bias_free")
        hi_dve = sem("hi_dve")
        hi_act = sem("hi_act")
        lo_dve = sem("lo_dve")
        lo_pool = sem("lo_pool")
        x_loaded = sem("x_loaded")
        xT_ps = sem("xT_ps")
        xhi_made = sem("xhi_made")
        xlo_made = sem("xlo_made")
        fc1_ps = sem("fc1_ps")
        t1_made = sem("t1_made")
        sl_made = sem("sl_made")
        u_made = sem("u_made")
        a_made = sem("a_made")
        aT_ps = sem("aT_ps")
        ahi_made = sem("ahi_made")
        alo_made = sem("alo_made")
        y_ps = sem("y_ps")
        y_out = sem("y_out")
        y_stored = sem("y_stored")
        got = [sem(f"got{t}") for t in range(NT)]
        summed = sem("summed")
        out_stored = sem("out_stored")
        tick = sem("tick")

        XT, Y = 6, 7
        bank = lambda i: ps[:, i, :]
        chunk = lambda w, c: w[:, c, :, :].rearrange("p k n -> p (k n)")
        y_tiles = y_dram.rearrange("(g p) d -> g p d", p=P)
        x_tiles = rows_dram.rearrange("(g p) d -> g p d", p=P)
        yg = raw[:, :, :].rearrange("p c n -> p (c n)")[:, 0:TOP * NT * D].rearrange(
            "p (t k d) -> p t k d", t=NT, k=TOP)

        def hi_ready(eng, e, c):
            if c == 0:
                eng.wait_ge(hi_dve, e + 1)
            else:
                eng.wait_ge(hi_act, (CH - 1) * e + ACT_CHUNKS.index(c) + 1)

        def lo_ready(eng, e, c):
            if c < 3:
                eng.wait_ge(lo_dve, 3 * e + c + 1)
            else:
                eng.wait_ge(lo_pool, 3 * e + c - 2)

        def tiles(eng, e):
            first = eng.value_load(gstart[0:1, bass.ds(e, 1)], min_val=0, max_val=MAXT - 1)
            last = eng.value_load(gstart[0:1, bass.ds(e + 1, 1)], min_val=1, max_val=MAXT)
            return first, last

        block = ctx.enter_context(nc.Block())

        @block.sync
        def _(sp):
            def load_bias(e):
                sp.dma_start(bias[:, :, :, :].rearrange("p q g n -> p (q g n)"),
                             fc1b[bass.ds(e, 1), :].rearrange("a n -> (a n)").partition_broadcast(P))\
                  .then_inc(bias_in, 16)

            load_bias(0)
            with sp.Fori(0, EX - 1) as e:
                for c in range(CH):
                    hi_ready(sp, e, c)
                    sp.sem_inc(tick, 1)
                    lo_ready(sp, e, c)
                    sp.sem_inc(tick, 1)
                    sp.dma_start(raw[:, c, :], wall[bass.ds(e * CH + CH + c, 1), :, :]
                                 .rearrange("a p n -> (a p) n")).then_inc(raw_in[c], 16)
                sp.wait_ge(bias_free, e + 1)
                load_bias(e + 1)
            for t in range(NT):
                n = P if t < NT - 1 else TAIL
                sp.wait_ge(summed, TOP * (t + 1))
                sp.dma_start(out[t * P:t * P + n, :], xres[0:n, t, :]).then_inc(out_stored, 16)
            sp.wait_ge(out_stored, 16 * NT)

        @block.gpsimd
        def _(pool):
            with pool.Fori(0, EX) as e:
                for c in (3, 4, 5):
                    hi_ready(pool, e, c)
                    pool.tensor_tensor(chunk(wlo, c), raw[:, c, :], chunk(whi, c), ALU.subtract)\
                        .then_inc(lo_pool, 1)
            total = pool.value_load(gstart[0:1, EX:EX + 1], min_val=1, max_val=MAXT)
            pool.wait_ge(y_stored, 16 * total + 16)
            pool.sem_inc(tick, 1)
            for t in range(NT):
                n = P if t < NT - 1 else TAIL
                for k in range(TOP):
                    pool.indirect_dma_start(
                        yg[0:n, t, k, :], None, y_dram,
                        bass.IndirectOffsetOnAxis(yslots[0:n, k, t:t + 1], 0)).then_inc(got[t], 16)

        @block.tensor
        def _(pe):
            def transposes(to, of):
                for k in range(KD):
                    tr = pe.transpose(to[:, k * P:(k + 1) * P], of[:, k * P:(k + 1) * P], ident[:, :])
                return tr

            pe.wait_ge(x_loaded, 16)
            transposes(bank(Y), xg[:, :]).then_inc(y_ps, 1)
            transposes(bank(XT), xg[:, :]).then_inc(xT_ps, 1)
            pe.sem_inc(fc1_ps, 1)

            def product(o, hi, lo, c, e=None, part=(0, 3 * KD), start=True, stop=True):
                steps = [(k, l, w) for l, w in ((hi, whi), (lo, whi), (hi, wlo)) for k in range(KD)]
                for n in range(*part):
                    if n == 0:
                        hi_ready(pe, e, c)
                    if n == 2 * KD:
                        lo_ready(pe, e, c)
                    k, l, w = steps[n]
                    mm = pe.matmul(o, l[:, k, :], w[:, c, k, :], start=start and n == 0,
                                   stop=stop and n == len(steps) - 1)
                return mm

            with pe.Fori(0, EX) as e:
                first, last = tiles(pe, e)
                with pe.Fori(first, last) as g:
                    def turn(q):
                        pe.wait_ge(a_made, 2 * g + q + 1)
                        transposes(bank(4 + q), a[:, q, :]).then_inc(aT_ps, 1)

                    pe.wait_ge(xhi_made, g + 1)
                    product(bank(0), xhi, xlo, 0, e, (0, KD), stop=False)
                    pe.wait_ge(xlo_made, g + 1)
                    product(bank(0), xhi, xlo, 0, e, (KD, 3 * KD)).then_inc(fc1_ps, 1)
                    for c in (1, 2):
                        product(bank(c), xhi, xlo, c, e).then_inc(fc1_ps, 1)
                    product(bank(3), xhi, xlo, 3, e, (0, KD), stop=False)
                    turn(0)
                    product(bank(3), xhi, xlo, 3, e, (KD, 3 * KD)).then_inc(fc1_ps, 1)
                    pe.wait_ge(ahi_made, 2 * g + 1)
                    pe.wait_ge(alo_made, 2 * g + 1)
                    pe.wait_ge(y_out, g + 1)
                    product(bank(Y), ahi[:, 0, :, :], alo[:, 0, :, :], 4, e, (0, 7), stop=False)
                    turn(1)
                    product(bank(Y), ahi[:, 0, :, :], alo[:, 0, :, :], 4, e, (7, 3 * KD), stop=False)
                    pe.wait_ge(x_loaded, 16 * g + 32)
                    transposes(bank(XT), xg[:, :]).then_inc(xT_ps, 1)
                    pe.wait_ge(ahi_made, 2 * g + 2)
                    product(bank(Y), ahi[:, 1, :, :], alo[:, 1, :, :], 5, e, (0, KD), start=False, stop=False)
                    pe.wait_ge(alo_made, 2 * g + 2)
                    product(bank(Y), ahi[:, 1, :, :], alo[:, 1, :, :], 5, e, (KD, 3 * KD), start=False)\
                        .then_inc(y_ps, 1)

        @block.scalar
        def _(act):
            def load_x(g):
                act.dma_start(xg[:, :], x_tiles[bass.ds(g, 1), :, :].rearrange("a p d -> (a p) d"))\
                   .then_inc(x_loaded, 16)

            def store_y(g):
                act.wait_ge(y_ps, g + 1)
                act.activation(ysb[:, :], bank(Y), ACT.Copy).then_inc(y_out, 1)
                act.wait_ge(y_out, g + 1)
                act.dma_start(y_tiles[bass.ds(g, 1), :, :].rearrange("a p d -> (a p) d"), ysb[:, :])\
                   .then_inc(y_stored, 16)

            def copy_x(n):
                act.wait_ge(xT_ps, n)
                act.activation(xhi[:, :, :].rearrange("p k n -> p (k n)"), bank(XT), ACT.Copy)\
                   .then_inc(xhi_made, 1)

            act.dma_start(xg[:, :], x_tiles[0, :, :]).then_inc(x_loaded, 16)
            copy_x(1)
            act.preload_act_table(ACT.Silu)
            with act.Fori(0, EX) as e:
                for c in ACT_CHUNKS:
                    if c == 4:
                        first, last = tiles(act, e)
                        act.wait_ge(y_ps, first + 1)
                    act.wait_ge(raw_in[c], 16 * e + 16)
                    act.activation(chunk(whi, c), raw[:, c, :], ACT.Copy).then_inc(hi_act, 1)
                with act.Fori(first, last) as g:
                    act.wait_ge(xT_ps, g + 1)
                    load_x(g + 1)
                    store_y(g)
                    for q in range(2):
                        act.wait_ge(t1_made, 2 * g + q + 1)
                        act.activation(sl[:, q, :], t1[:, q, :], ACT.Silu).then_inc(sl_made, 1)
                        act.wait_ge(aT_ps, 2 * g + q + 1)
                        act.activation(ahi[:, q, :, :].rearrange("p k n -> p (k n)"), bank(4 + q), ACT.Copy)\
                           .then_inc(ahi_made, 1)
                    copy_x(g + 2)
                    act.wait_ge(y_stored, 16 * g + 16)
                    act.sem_inc(tick, 1)
            total = act.value_load(gstart[0:1, EX:EX + 1], min_val=1, max_val=MAXT)
            store_y(total)
            act.wait_ge(y_stored, 16 * total + 16)
            act.sem_inc(tick, 1)

        @block.vector
        def _(v):
            def lower_x(n):
                v.wait_ge(xhi_made, n)
                v.tensor_tensor(xlo[:, :, :].rearrange("p k n -> p (k n)"), bank(XT),
                                xhi[:, :, :].rearrange("p k n -> p (k n)"), ALU.subtract).then_inc(xlo_made, 1)

            lower_x(1)
            with v.Fori(0, EX) as e:
                v.wait_ge(raw_in[0], 16 * e + 16)
                v.tensor_copy(chunk(whi, 0), raw[:, 0, :]).then_inc(hi_dve, 1)
                for c in range(3):
                    if c == 2:
                        v.wait_ge(bias_in, 16 * e + 16)
                    hi_ready(v, e, c)
                    v.tensor_tensor(chunk(wlo, c), raw[:, c, :], chunk(whi, c), ALU.subtract).then_inc(lo_dve, 1)
                first, last = tiles(v, e)
                with v.Fori(first, last) as g:
                    def gate(q):
                        v.wait_ge(fc1_ps, 4 * g + 2 * q + 2)
                        v.tensor_tensor(t1[:, q, :], bank(2 * q), bias[:, q, 0, :], ALU.add).then_inc(t1_made, 1)

                    def up(q):
                        v.wait_ge(fc1_ps, 4 * g + 2 * q + 3)
                        v.tensor_tensor(a[:, q, :], bank(2 * q + 1), bias[:, q, 1, :], ALU.add)\
                         .then_inc(u_made, 1)
                        v.wait_ge(u_made, 2 * g + q + 1)
                        v.wait_ge(sl_made, 2 * g + q + 1)
                        v.tensor_tensor(a[:, q, :], a[:, q, :], sl[:, q, :], ALU.mult).then_inc(a_made, 1)

                    def lower_a(q):
                        v.wait_ge(ahi_made, 2 * g + q + 1)
                        v.tensor_tensor(alo[:, q, :, :].rearrange("p k n -> p (k n)"), bank(4 + q),
                                        ahi[:, q, :, :].rearrange("p k n -> p (k n)"), ALU.subtract)\
                         .then_inc(alo_made, 1)

                    gate(0)
                    up(0)
                    gate(1)
                    lower_a(0)
                    up(1)
                    lower_a(1)
                    lower_x(g + 2)
                v.sem_inc(bias_free, 1)
            for t in range(NT):
                n = P if t < NT - 1 else TAIL
                v.wait_ge(got[t], 16 * TOP)
                for k in range(TOP):
                    f = v.scalar_tensor_tensor(xres[0:n, t, :], yg[0:n, t, k, :], wts[0:n, k, t:t + 1],
                                               xres[0:n, t, :], ALU.mult, ALU.add)
                    f.then_inc(summed, 1)
                    v.wait_ge(summed, TOP * t + k + 1)


def kernel(**inputs):
    import numpy as np
    import concourse.bacc as bacc
    from concourse.bass_utils import run_bass_kernel_spmd

    arr = {k: np.asarray(v) for k, v in inputs.items()}

    def edges(a, pad):
        whole = np.full(ET * P, pad, np.int32)
        whole[:EDGES] = a
        return np.ascontiguousarray(whole.reshape(ET, P).T)

    fc1 = arr["L0_ffn_fc1_w"].reshape(EX, 2, 2, D, KD, P).transpose(0, 2, 1, 5, 4, 3).reshape(EX, 4, P, CW)
    fc2 = arr["L0_ffn_fc2_w"].reshape(EX, D, 2, KD, P).transpose(0, 2, 4, 3, 1).reshape(EX, 2, P, CW)
    arrays = {
        "x": arr["x"],
        "src": edges(arr["src"], 0),
        "dst": edges(arr["dst"], NO_NODE),
        "W1": arr["L0_gnn_W1"],
        "b1": np.ascontiguousarray(arr["L0_gnn_b1"].reshape(KD, P).T),
        "W2": arr["L0_gnn_W2"],
        "b2": arr["L0_gnn_b2"],
        "rw": np.ascontiguousarray(arr["L0_ffn_router_w"].T),
        "rb": arr["L0_ffn_router_b"],
        "wall": np.ascontiguousarray(np.concatenate([fc1, fc2], axis=1).reshape(EX * CH, P, CW)),
        "fc1b": np.ascontiguousarray(
            arr["L0_ffn_fc1_b"].reshape(EX, 2, 2, D).transpose(0, 2, 1, 3).reshape(EX, 4 * D)),
        "fc2b": arr["L0_ffn_fc2_b"],
    }
    nc = bacc.Bacc("TRN2", target_bir_lowering=False, num_devices=1)
    args = [nc.dram_tensor(f"in_{k}", a.shape, mybir.dt.from_np(a.dtype), kind="ExternalInput").ap()
            for k, a in arrays.items()]
    out = nc.dram_tensor("out", (N, D), F32, kind="ExternalOutput").ap()
    build(nc, *args, out)
    r = run_bass_kernel_spmd(nc, [{f"in_{k}": a for k, a in arrays.items()}], core_ids=[0])
    return r.results[0]["out"]
```

```python
from contextlib import ExitStack

import concourse.bass as bass
from concourse import mybir

F32 = mybir.dt.float32
F32R = mybir.dt.float32r
BF16 = mybir.dt.bfloat16
FP8 = mybir.dt.float8e4
FP16 = mybir.dt.float16
I32 = mybir.dt.int32
ALU = mybir.AluOpType
ACT = mybir.ActivationFunctionType
AX = mybir.AxisListType

P = 128
N = 1250
D = 512
EDGES = 20000
NT = -(-N // P)
NP = NT * P
TAIL = N - (NT - 1) * P
EG = 4
GE = -(-EDGES // (EG * P))
ET = EG * GE
KD = D // P
EX = 8
TOP = 2
HID = 1024
CH = 6
PARTS_AT = (1, 3, 4, 6, 7, 8, 9)
ACT_CHUNKS = (1, 3, 2, 4, 5)
CW = KD * D
MAXT = (TOP * N + (P - 1) * EX + EX) // P
META = 4
ROW = D + META
EPS = 1e-5
NO_NODE = 4095


def build(nc, x, src, dst, W1, b1, W2, b2, rw, rb, wall, fc1b, fc2b, out):
    rows_dram = nc.dram_tensor("expert_rows", ((MAXT + 1) * P, ROW), F32).ap()

    with ExitStack() as ctx:
        def sb(name, shape, dt, c=ctx):
            return c.enter_context(nc.sbuf_tensor(name, shape, dt))

        def sem(name):
            return ctx.enter_context(nc.semaphore(name))

        ps = ctx.enter_context(nc.psum_tensor("ps", [P, 8, 512], F32))
        ident = sb("ident", [P, P], F32)
        xres = sb("xres", [P, NT, D], F32)
        gstart = sb("gstart", [1, EX + 1], I32)

        with nc.sbuf_tensor("raw", [P, CH, CW], F32) as raw:
            pass

        raw_in = [sem(f"raw_in{c}") for c in range(CH)]
        scattered = sem("scattered")
        out_stored = sem("out_stored")
        graph_block(nc, ctx, locals())
        expert_block(nc, ctx, locals())


def graph_block(nc, outer, env):
    x, src, dst, W1, b1, W2, b2, rw, rb, wall, fc2b, out = (env[k] for k in (
        "x", "src", "dst", "W1", "b1", "W2", "b2", "rw", "rb", "wall", "fc2b", "out"))
    ident, xres, raw, gstart, ps = (env[k] for k in ("ident", "xres", "raw", "gstart", "ps"))
    raw_in, scattered, out_stored, rows_dram = (env[k] for k in ("raw_in", "scattered", "out_stored", "rows_dram"))

    with ExitStack() as ctx:
        def sb(name, shape, dt):
            return ctx.enter_context(nc.sbuf_tensor(name, shape, dt))

        def sem(name):
            return ctx.enter_context(nc.semaphore(name))

        with (nc.sbuf_tensor("hot_d", [P, ET, P], BF16) as hot_d,
              nc.sbuf_tensor("flags", [P, NT * ET], BF16) as flags):
            pass
        with (nc.sbuf_tensor("hhi", [P, NT, D], F32R) as hhi,
              nc.sbuf_tensor("hlo", [P, NT, D], F32R) as hlo,
              nc.sbuf_tensor("dis_bc", [P, NP], F32) as dis_bc):
            pass
        sb("raw_place", [P, CH, CW], F32)
        Cs = sb("Cs", [P, NP], F32)
        with nc.sbuf_tensor("CTx", [P, NT, NP], F32) as CTx:
            pass
        CT = sb("CT", [P, NT, NP], F32R)
        CTlo = sb("CTlo", [P, NT, NP], FP8)
        h = sb("h", [P, NT, D], F32)
        with (nc.sbuf_tensor("hot_s", [P, EG, NP], BF16) as hot_s,
              nc.sbuf_tensor("eyez", [P, 2 * NP], BF16) as eyez,
              nc.sbuf_tensor("iota", [P, NP], FP16) as iota,
              nc.sbuf_tensor("src_i", [P, ET], I32) as src_i,
              nc.sbuf_tensor("dst_i", [P, ET], I32) as dst_i):
            pass
        with nc.sbuf_tensor("ranges_row", [1, 2 * NP], F32) as spare:
            pass
        with nc.sbuf_tensor("h1T", [P, KD, NP], F32) as h1T:
            pass
        rows = sb("rows", [P, NT, ROW], F32)
        xn1 = rows[:, :, 0:D]
        blank = sb("blank", [P, ROW], F32)
        wts = sb("wts", [P, TOP, NT], F32)
        slots = sb("slots", [P, TOP, NT], I32)
        token = sb("token", [P, NT], F32)
        Wg = sb("Wg", [P, KD, D], F32)
        xn = sb("xn", [P, 2, D], F32)
        xnT = sb("xnT", [P, 2, KD, P], F32)
        b2_bc = sb("b2_bc", [P, D], F32)
        src_f = sb("src_f", [P, ET], F32)
        dst_f = sb("dst_f", [P, ET], FP16)
        blk_f = sb("blk_f", [P, ET], F32)
        src_m = sb("src_m", [P, ET], F32)
        many = sb("many", [P, 1], F32)
        many_b = sb("many_b", [P, 1], BF16)
        many_i = sb("many_i", [1, 1], I32)
        b1c = sb("b1c", [P, KD], F32)
        rwT = sb("rwT", [P, KD, EX], F32)
        rb_bc = sb("rb_bc", [P, EX], F32)
        stat = sb("stat", [P, 6], F32)
        mv = sb("mv", [P, NT, 2], F32)
        sd = sb("sd", [P, NT], F32)
        rs = sb("rs", [P, NT], F32)
        deg = sb("deg", [P, NT], F32)
        dis = sb("dis", [P, NT], F32)
        t4 = sb("t4", [P, 4, NT], F32)
        ones_b = sb("ones_b", [P, P], BF16)
        ones_f = sb("ones_f", [P, P], F32)
        below = sb("below", [P, P], BF16)
        lg = sb("lg", [P, NT, EX], F32)
        valid = sb("valid", [P, NT], F32)
        iota_e = sb("iota_e", [P, NT, EX], F32)
        sc8 = sb("sc8", [P, 2, NT, EX], F32)
        top = sb("top", [P, TOP, NT, EX], F32)
        mx = sb("mx", [P, 6, NT], F32)
        mem_b = sb("mem_b", [P, NT, EX], BF16)
        rank = sb("rank", [P, NT, EX], F32)
        e8 = sb("e8", [P, 6, EX], F32)
        thr = sb("thr", [P, EX, NT], F32)
        cmp8 = sb("cmp8", [P, EX, NT], F32)
        rng_i = sb("rng_i", [1, 2, NT], I32)
        h_flat = h[:, :, :].rearrange("p t d -> p (t d)")
        cwT = h_flat[0:EX, 0:NP].rearrange("p (t n) -> p t n", t=NT)
        fc2b_sb = h_flat[0:EX, NP:NP + D]

        edges_in = sem("edges_in")
        x_in = [sem(f"x_in{i}") for i in range(4)]
        w1_in = sem("w1_in")
        w2_in = sem("w2_in")
        consts_in = sem("consts_in")
        fc2b_in = sem("fc2b_in")
        zero_out = sem("zero_out")
        pool_made = sem("pool_made")
        flags_made = sem("flags_made")
        flags_summed = sem("flags_summed")
        ranges_made = sem("ranges_made")
        dve = sem("dve")
        var_made = sem("var_made")
        root_made = sem("root_made")
        xn_made = sem("xn_made")
        xnT_ps = sem("xnT_ps")
        xnT_made = sem("xnT_made")
        h_ps = sem("h_ps")
        h_made = sem("h_made")
        hot_d_made = sem("hot_d_made")
        hot_made = sem("hot_made")
        hot_free = sem("hot_free")
        counts_ps = sem("counts_ps")
        counts_out = sem("counts_out")
        ct_ps = sem("ct_ps")
        ct_made = sem("ct_made")
        ct_copied = sem("ct_copied")
        ctlo_made = sem("ctlo_made")
        whole_made = sem("whole_made")
        diag_made = sem("diag_made")
        disbc_ps = sem("disbc_ps")
        disbc_made = sem("disbc_made")
        dis_made = sem("dis_made")
        many_summed = sem("many_summed")
        many_found = sem("many_found")
        hhi_made = sem("hhi_made")
        hlo_made = sem("hlo_made")
        agg1_ps = sem("agg1_ps")
        agg1_scaled = sem("agg1_scaled")
        h1T_made = sem("h1T_made")
        agg2_ps = sem("agg2_ps")
        agg2_out = sem("agg2_out")
        lg_ps = sem("lg_ps")
        mem_made = sem("mem_made")
        rank_ps = sem("rank_ps")
        slots_made = sem("slots_made")
        cw_made = sem("cw_made")
        cwT_ps = sem("cwT_ps")
        cwT_made = sem("cwT_made")
        eb_ps = sem("eb_ps")

        GROUPS = [(0, 512), (512, 1024), (1024, NP)]
        bank = lambda i: ps[:, i, :]
        flat = ps[:, :, :].rearrange("p b n -> p (b n)")

        block = ctx.enter_context(nc.Block())

        @block.sync
        def _(sp):
            sp.dma_start(dst_i[:, :], dst).then_inc(edges_in, 16)
            sp.dma_start(src_i[:, :], src).then_inc(edges_in, 16)
            xt = x[0:(NT - 1) * P, :].rearrange("(t p) d -> p t d", p=P)
            for i in range(3):
                sp.dma_start(xres[:, 3 * i:3 * i + 3, :], xt[:, 3 * i:3 * i + 3, :]).then_inc(x_in[i], 16)
            sp.dma_start(Wg[:, :, :], W1.rearrange("(k p) n -> p k n", p=P)).then_inc(w1_in, 16)
            sp.wait_ge(pool_made, 1)
            sp.dma_start(xres[0:TAIL, NT - 1, :], x[(NT - 1) * P:N, :]).then_inc(x_in[3], 16)
            sp.dma_start(b1c[:, :], b1).then_inc(consts_in, 16)
            sp.dma_start(rwT[:, :, :], rw.rearrange("(k p) e -> p k e", p=P)).then_inc(consts_in, 16)
            sp.dma_start(rb_bc[:, :], rb.partition_broadcast(P)).then_inc(consts_in, 16)
            sp.dma_start(b2_bc[:, :], b2.partition_broadcast(P)).then_inc(consts_in, 16)
            sp.wait_ge(pool_made, 18)
            for g in range(MAXT + 1):
                sp.dma_start(rows_dram[g * P:(g + 1) * P, :], blank[:, :]).then_inc(zero_out, 16)
            sp.dma_start(out[N:N + P, :], blank[:, 0:D]).then_inc(out_stored, 16)
            sp.wait_ge(h_ps, NT)
            sp.dma_start(Wg[:, :, :], W2.rearrange("(k p) n -> p k n", p=P)).then_inc(w2_in, 16)
            sp.wait_ge(hhi_made, NT)
            sp.wait_ge(hlo_made, NT)
            sp.dma_start(fc2b_sb, fc2b).then_inc(fc2b_in, 16)
            sp.wait_ge(agg2_ps, NT)
            for c in range(CH):
                sp.dma_start(raw[:, c, :], wall[c, :, :]).then_inc(raw_in[c], 16)
            for t in range(NT):
                n = P if t < NT - 1 else TAIL
                sp.wait_ge(agg2_out, NT + t + 1)
                sp.dma_start(out[t * P:t * P + n, :], xres[0:n, t, :]).then_inc(out_stored, 16)

        @block.gpsimd
        def _(pool):
            made = 0

            def step(ins):
                nonlocal made
                made += 1
                ins.then_inc(pool_made, 1)
                pool.wait_ge(pool_made, made)

            step(pool.memset(xres[:, NT - 1, :], 0.0))
            step(pool.memset(eyez[:, :], 0.0))
            mid = eyez[:, NP - P:NP]
            step(pool.affine_select(out=mid, in_=mid, compare_op=ALU.not_equal, fill=1.0, base=0,
                                    pattern=[[-1, P]], channel_multiplier=1))
            step(pool.memset(ident[:, :], 0.0))
            step(pool.affine_select(out=ident[:, :], in_=ident[:, :], compare_op=ALU.not_equal, fill=1.0,
                                    base=0, pattern=[[-1, P]], channel_multiplier=1))
            step(pool.memset(ones_b[:, :], 1.0))
            step(pool.iota(iota[:, :], pattern=[[1, NP]], base=1, channel_multiplier=0,
                           allow_small_or_imprecise_dtypes=True))
            step(pool.iota(spare[0:1, 0:GE], pattern=[[1, GE]], base=1, channel_multiplier=0,
                           allow_small_or_imprecise_dtypes=True))
            step(pool.iota(spare[0:1, GE:2 * GE], pattern=[[-1, GE]], base=GE, channel_multiplier=0,
                           allow_small_or_imprecise_dtypes=True))
            step(pool.memset(ones_f[:, :], 1.0))
            step(pool.affine_select(out=below[:, :], in_=ones_b[:, :], compare_op=ALU.is_gt, fill=0.0,
                                    base=0, pattern=[[1, P]], channel_multiplier=-1))
            step(pool.memset(valid[:, :], 1.0))
            step(pool.affine_select(out=valid[:, :], in_=valid[:, :], compare_op=ALU.is_gt, fill=0.0,
                                    base=N, pattern=[[-P, NT]], channel_multiplier=-1))
            step(pool.iota(iota_e[:, :, :], pattern=[[0, NT], [1, EX]], base=-EX, channel_multiplier=0,
                           allow_small_or_imprecise_dtypes=True))
            step(pool.iota(thr[:, :, :], pattern=[[0, EX], [P, NT]], base=0, channel_multiplier=0,
                           allow_small_or_imprecise_dtypes=True))
            step(pool.memset(blank[:, :], 0.0))
            step(pool.iota(blank[:, D:D + 1], pattern=[[0, 1]], base=N, channel_multiplier=1,
                           allow_small_or_imprecise_dtypes=True))
            step(pool.iota(token[:, :], pattern=[[P, NT]], base=0, channel_multiplier=1,
                           allow_small_or_imprecise_dtypes=True))
            for n in range(3 * NT):
                b, q = n // 3, n % 3
                m = min(4, NT - 4 * q)
                pool.wait_ge(ct_copied, n + 1)
                pool.wait_ge(ct_made, n + 1)
                pool.tensor_tensor(CTlo[:, 4 * q:4 * q + m, b * P:(b + 1) * P],
                                   xn[:, n % 2, 0:m * P].rearrange("p (k n) -> p k n", k=m),
                                   CT[:, 4 * q:4 * q + m, b * P:(b + 1) * P], ALU.subtract, saturate=False)\
                    .then_inc(ctlo_made, 1)
            pool.wait_ge(zero_out, 16 * (MAXT + 1))
            pool.wait_ge(slots_made, 1)
            for t in range(NT):
                n = P if t < NT - 1 else TAIL
                for k in range(TOP):
                    pool.indirect_dma_start(
                        rows_dram, bass.IndirectOffsetOnAxis(slots[0:n, k, t:t + 1], 0),
                        rows[0:n, t, :], None).then_inc(scattered, 16)
            pool.wait_ge(scattered, 16 * NT * TOP)

        @block.tensor
        def _(pe):
            pe.wait_ge(flags_made, 1)
            pe.wait_ge(pool_made, 6)
            for a in range(0, NT * ET, 512):
                b = min(a + 512, NT * ET)
                mm = pe.matmul(flat[0:1, a:b], ones_b[:, 0:1], flags[:, a:b], start=True, stop=True)
            mm.then_inc(flags_summed, 1)

            def either(large, products):
                with pe.If(large != 0):
                    pe.wait_ge(whole_made, NT)
                    products(CTx, lambda part: part.bitcast(F32))
                with pe.Else():
                    products(CT, lambda part: part)

            def transposes(t, of, to):
                for k in range(KD):
                    tr = pe.transpose(to[:, k * P:(k + 1) * P], of[:, k * P:(k + 1) * P], ident[:, :])
                return tr

            for t in range(NT + 1):
                if t < NT:
                    pe.wait_ge(xn_made, t + 1)
                    if t >= 2:
                        pe.wait_ge(xnT_made, t - 1)
                    transposes(t, xn[:, t % 2, :], bank(6 + t % 2)).then_inc(xnT_ps, 1)
                if t >= 1:
                    s = t - 1
                    if s == 0:
                        pe.wait_ge(w1_in, 16)
                    pe.wait_ge(xnT_made, s + 1)
                    if s >= 2:
                        pe.wait_ge(h_made, s - 1)
                    for k in range(KD):
                        mm = pe.matmul(bank(4 + s % 2), xnT[:, s % 2, k, :], Wg[:, k, :],
                                       start=(k == 0), stop=(k == KD - 1))
                    mm.then_inc(h_ps, 1)

            n_hot = pe.alloc_register("pe_hot")
            pe.reg_mov(n_hot, 0)
            pe.wait_ge(ranges_made, 1)
            pe.wait_ge(hot_d_made, len(PARTS_AT))
            pe.sem_inc(hot_free, EG)

            def ct_block(b, parts):
                for q in parts:
                    if q == 0:
                        pe.wait_ge(counts_out, b + 1)
                    n = 3 * b + q
                    if n >= 2:
                        pe.wait_ge(ct_made, n - 1)
                    for k in range(4 * q, min(4 * q + 4, NT)):
                        tr = pe.transpose(bank(6 + n % 2)[:, (k % 4) * P:(k % 4 + 1) * P],
                                          Cs[:, k * P:(k + 1) * P], ident[:, :])
                    tr.then_inc(ct_ps, 1)

            for b in range(NT):
                first = pe.value_load(rng_i[0:1, 0, b:b + 1], min_val=0, max_val=GE - 1)
                last = pe.value_load(rng_i[0:1, 1, b:b + 1], min_val=1, max_val=GE)
                o = flat[:, 1536 * (b % 2):1536 * (b % 2) + NP + 1]
                if b == 1:
                    pe.wait_ge(h_made, NT)
                if b >= 2:
                    pe.wait_ge(counts_out, b - 1)
                at = NP - P - b * P
                for lo, hi in ((0, 512), (512, 1024), (1024, NP + 1)):
                    pe.matmul(o[:, lo:hi], eyez[:, NP - P:NP], eyez[:, at + lo:at + hi],
                              start=True, stop=False, skip_group_check=True)
                if b >= 2:
                    ct_block(b - 2, (2,))
                with pe.Fori(first, last) as i:
                    for j in range(EG):
                        pe.reg_add(n_hot, n_hot, 1)
                        pe.wait_ge(hot_made, n_hot)
                        to_tile = hot_d[:, bass.ds(EG * i + j, 1), :].rearrange("p a n -> p (a n)")
                        source = hot_s[:, j, :]
                        for lo, hi in GROUPS:
                            pe.matmul(o[:, lo:hi], to_tile, source[:, lo:hi],
                                      start=False, stop=False, skip_group_check=True)
                        pe.matmul(o[:, NP:NP + 1], to_tile, flags[:, bass.ds(EG * i + (b * ET + j), 1)],
                                  start=False, stop=False, skip_group_check=True).then_inc(hot_free, 1)
                pe.matmul(o[:, 0:1], eyez[:, NP - P:NP], eyez[:, 0:1], start=False, stop=True,
                          skip_group_check=True).then_inc(counts_ps, 1)
                if b >= 1:
                    ct_block(b - 1, (0, 1))
            ct_block(NT - 2, (2,))
            ct_block(NT - 1, (0, 1, 2))

            pe.wait_ge(dis_made, 1)
            pe.matmul(bank(5)[0:1, 0:1], many_b[:, :], ones_b[:, 0:1], start=True, stop=True)\
              .then_inc(many_summed, 1)
            pe.wait_ge(pool_made, 10)
            for t in range(NT):
                pe.wait_ge(diag_made, t + 1)
                mm = pe.matmul(flat[:, t * P:(t + 1) * P], ones_f[:, :], xnT[:, t % 2, 0, :],
                               start=(t % 4 == 0), stop=True, skip_group_check=True)
                mm.then_inc(disbc_ps, 1)
            pe.wait_ge(ct_made, 3 * NT)
            pe.wait_ge(many_found, 1)
            large = pe.value_load(many_i[0:1, 0:1], min_val=0, max_val=1)

            def aggregate1(counts, view):
                n = 0
                for lo, hi in GROUPS:
                    for j in range(KD):
                        if n >= 2:
                            pe.wait_ge(agg1_scaled, n - 1)
                        for i in range(2 * NT):
                            k, part = i % NT, (hhi, hlo)[i // NT]
                            if n == 0:
                                pe.wait_ge((hhi_made, hlo_made)[i // NT], k + 1)
                            mm = pe.matmul(bank(3 + n % 2)[:, 0:hi - lo], view(part[:, k, j * P:(j + 1) * P]),
                                           counts[:, k, lo:hi], start=(i == 0), stop=(i == 2 * NT - 1))
                        mm.then_inc(agg1_ps, 1)
                        n += 1

            either(large, aggregate1)
            pe.wait_ge(w2_in, 16)
            for m in range(NT):
                pe.wait_ge(h1T_made, KD * (m // 4 + 1))
                if m >= 2:
                    pe.wait_ge(hhi_made, NT + m - 1)
                    pe.wait_ge(hlo_made, NT + m - 1)
                for k in range(KD):
                    mm = pe.matmul(bank(5 + m % 2), h1T[:, k, m * P:(m + 1) * P], Wg[:, k, :],
                                   start=(k == 0), stop=(k == KD - 1))
                mm.then_inc(h_ps, 1)
            pe.wait_ge(disbc_made, 1)

            def aggregate2(counts, view):
                for m in range(NT + 2):
                    if m < NT:
                        if m >= 2:
                            pe.wait_ge(agg2_out, m - 1)
                        for i in range(2 * NT):
                            k, part = i % NT, (hhi, hlo)[i // NT]
                            if m == 0:
                                pe.wait_ge((hhi_made, hlo_made)[i // NT], NT + k + 1)
                            mm = pe.matmul(bank(3 + m % 2), counts[:, k, m * P:(m + 1) * P],
                                           view(part[:, k, :]), start=(i == 0), stop=(i == 2 * NT - 1))
                        mm.then_inc(agg2_ps, 1)
                    if 1 <= m <= NT:
                        s = m - 1
                        pe.wait_ge(xn_made, NT + s + 1)
                        transposes(s, xn1[:, s, :], bank(6 + s % 2)).then_inc(xnT_ps, 1)
                    if m >= 2:
                        s = m - 2
                        pe.wait_ge(xnT_made, NT + s + 1)
                        for k in range(KD):
                            mm = pe.matmul(bank(1)[:, s * EX:(s + 1) * EX], xnT[:, s % 2, k, :], rwT[:, k, :],
                                           start=(k == 0 and s == 0), stop=(k == KD - 1), skip_group_check=True)
                        mm.then_inc(lg_ps, 1)

            either(large, aggregate2)

            pe.wait_ge(mem_made, 1)
            mem = mem_b[:, :, :].rearrange("p t e -> p (t e)")
            pe.matmul(bank(2)[:, 0:NT * EX], below[:, :], mem, start=True, stop=False, skip_group_check=True)
            for s in range(1, NT):
                mm = pe.matmul(bank(2)[:, s * EX:NT * EX], ones_b[:, :], mem[:, 0:(NT - s) * EX],
                               start=False, stop=(s == NT - 1), skip_group_check=True)
            for t in range(NT):
                mm = pe.matmul(bank(5)[:, 0:EX], ones_b[:, :], mem_b[:, t, :], start=(t == 0),
                               stop=(t == NT - 1))
            mm.then_inc(rank_ps, 1)
            pe.wait_ge(fc2b_in, 16)
            pe.wait_ge(cw_made, 1)
            for t in range(NT + 2):
                if t < NT:
                    if t >= 2:
                        pe.wait_ge(cwT_made, t - 1)
                    pe.transpose(bank(6 + t % 2)[0:EX, 0:P], sc8[:, 0, t, :], ident[:, :]).then_inc(cwT_ps, 1)
                if t >= 2:
                    q = t - 2
                    pe.wait_ge(cwT_made, q + 1)
                    if q >= 3:
                        pe.wait_ge(agg2_out, NT + q - 2)
                    pe.matmul(bank((3, 4, 0)[q % 3]), cwT[:, q, :], fc2b_sb, start=True, stop=True)\
                      .then_inc(eb_ps, 1)

        @block.scalar
        def _(act):
            def root(n, to, of):
                act.wait_ge(var_made, n)
                act.activation(to, of, ACT.Sqrt).then_inc(root_made, 1)

            root(1, sd[:, 0:3], mv[:, 0:3, 1])
            for t in range(NT + 1):
                if t in (1, 4, 7):
                    g = (t + 2) // 3
                    root(g + 1, sd[:, 3 * g:min(3 * g + 3, NT)], mv[:, 3 * g:min(3 * g + 3, NT), 1])
                if t < NT:
                    act.wait_ge(xnT_ps, t + 1)
                    if t >= 2:
                        act.wait_ge(h_ps, t - 1)
                    act.activation(xnT[:, t % 2, :, :].rearrange("p k n -> p (k n)"), bank(6 + t % 2),
                                   ACT.Copy).then_inc(xnT_made, 1)
                if t >= 1:
                    act.wait_ge(h_ps, t)
                    act.activation(h[:, t - 1, :], bank(4 + (t - 1) % 2), ACT.Copy).then_inc(h_made, 1)

            def ct_block(b):
                for q in range(3):
                    n = 3 * b + q
                    m = min(4, NT - 4 * q)
                    act.wait_ge(ct_ps, n + 1)
                    if n >= 2:
                        act.wait_ge(ctlo_made, n - 1)
                    act.activation(xn[:, n % 2, 0:m * P], bank(6 + n % 2)[:, 0:m * P], ACT.Copy)\
                       .then_inc(ct_copied, 1)
                    act.activation(CT[:, 4 * q:4 * q + m, b * P:(b + 1) * P],
                                   bank(6 + n % 2)[:, 0:m * P].rearrange("p (k n) -> p k n", k=m),
                                   ACT.Copy).then_inc(ct_made, 1)

            for b in range(NT):
                act.wait_ge(counts_ps, b + 1)
                if b >= 1:
                    ct_needed = 3 * b
                    act.wait_ge(ct_ps, ct_needed)
                act.activation(deg[:, b:b + 1], flat[:, 1536 * (b % 2) + NP:1536 * (b % 2) + NP + 1], ACT.Copy)
                act.activation(Cs[:, :], flat[:, 1536 * (b % 2):1536 * (b % 2) + NP], ACT.Copy)\
                   .then_inc(counts_out, 1)
                ct_block(b)

            root(5, sd[:, :], t4[:, 3, :])
            act.wait_ge(dis_made, 1)
            for t in range(NT):
                act.activation(hhi[:, t, :], h[:, t, :], ACT.Copy, scale=dis[:, t:t + 1]).then_inc(hhi_made, 1)
            act.wait_ge(disbc_ps, NT)
            act.activation(dis_bc[:, :], flat[:, 0:NP], ACT.Copy).then_inc(disbc_made, 1)
            act.wait_ge(consts_in, 64)
            n = 0
            for lo, hi in GROUPS:
                for j in range(KD):
                    act.wait_ge(agg1_scaled, n + 1)
                    act.activation(h1T[:, j, lo:hi], h1T[:, j, lo:hi], ACT.Relu, bias=b1c[:, j:j + 1])\
                       .then_inc(h1T_made, 1)
                    n += 1
            for m in range(NT):
                act.wait_ge(h_ps, NT + m + 1)
                if m == 0:
                    act.wait_ge(agg1_ps, 3 * KD)
                act.activation(hhi[:, m, :], bank(5 + m % 2), ACT.Copy, scale=dis[:, m:m + 1])\
                   .then_inc(hhi_made, 1)
            for m in range(NT):
                root(6 + m, sd[:, m:m + 1], mv[:, m, 1:2])
                act.wait_ge(xnT_ps, NT + m + 1)
                if m >= 2:
                    act.wait_ge(lg_ps, m - 1)
                act.activation(xnT[:, m % 2, :, :].rearrange("p k n -> p (k n)"), bank(6 + m % 2),
                               ACT.Copy).then_inc(xnT_made, 1)
            act.wait_ge(var_made, 6 + NT)
            act.activation(mx[:, 3, :], mx[:, 2, :], ACT.Exp).then_inc(root_made, 1)
            for t in range(NT):
                act.wait_ge(cwT_ps, t + 1)
                act.activation(cwT[:, t, :], bank(6 + t % 2)[0:EX, 0:P], ACT.Copy).then_inc(cwT_made, 1)

        @block.vector
        def _(v):
            done = 0

            def link(ins):
                nonlocal done
                done += 1
                ins.then_inc(dve, 1)
                v.wait_ge(dve, done)

            v.wait_ge(edges_in, 32)
            link(v.tensor_scalar(src_f[:, :], src_i[:, :], 1.0, None, ALU.add))
            link(v.tensor_scalar(src_i[:, :], dst_i[:, :], P - 1, None, ALU.bitwise_and))
            v.tensor_scalar(dst_f[:, :], src_i[:, :], 1.0, None, ALU.add)
            link(v.tensor_scalar(dst_i[:, :], dst_i[:, :], P.bit_length() - 1, None, ALU.arith_shift_right))
            link(v.tensor_scalar(blk_f[:, :], dst_i[:, :], 0.0, None, ALU.add))
            for b in range(NT):
                f = v.tensor_scalar(flags[:, b * ET:(b + 1) * ET], blk_f[:, :], float(b), None, ALU.is_equal)
            f.then_inc(flags_made, 1)

            def rsqrt(y, s, var, a, b):
                link(v.reciprocal(y, s))
                link(v.tensor_tensor(a, y, y, ALU.mult))
                link(v.tensor_tensor(b, a, var, ALU.mult))
                link(v.tensor_scalar(a, b, -0.5, 1.5, ALU.mult, ALU.add))
                link(v.tensor_tensor(y, y, a, ALU.mult))

            def stats(t):
                link(v.bn_stats(stat[:, :], xres[:, t, :]))
                link(v.bn_aggr(mv[:, t, :], stat[:, :]))

            def hot_d_part(i):
                a, b = ET * i // len(PARTS_AT), ET * (i + 1) // len(PARTS_AT)
                v.tensor_tensor(hot_d[:, a:b, :], iota[:, 0:P].unsqueeze(1).to_broadcast([P, b - a, P]),
                                dst_f[:, a:b].unsqueeze(2).to_broadcast([P, b - a, P]), ALU.is_equal)\
                 .then_inc(hot_d_made, 1)

            at = 2 * GE
            used, weighed = (spare[0:1, at + q * NT * GE:at + (q + 1) * NT * GE].rearrange(
                "p (b i) -> p b i", b=NT) for q in range(2))
            lim = spare[0:1, at + 2 * NT * GE:at + 2 * NT * GE + 3 * NT].rearrange("p (q b) -> p q b", b=NT)

            def groups_used():
                v.wait_ge(flags_summed, 1)
                v.wait_ge(pool_made, 9)
                link(v.tensor_reduce(used, flat[0:1, 0:NT * ET].rearrange("p (b i j) -> p b i j", j=EG, b=NT),
                                     AX.X, ALU.max))

            def ranges():
                for q in range(2):
                    weight = spare[0:1, q * GE:(q + 1) * GE].unsqueeze(1).to_broadcast([1, NT, GE])
                    link(v.scalar_tensor_tensor(weighed, used, 1.0, weight, ALU.min, ALU.mult))
                    link(v.tensor_reduce(lim[:, q, :], weighed, AX.X, ALU.max))
                link(v.tensor_scalar(lim[:, 0, :], lim[:, 0, :], 1.0, None, ALU.max))
                link(v.tensor_scalar(lim[:, 1, :], lim[:, 1, :], -1.0, float(GE), ALU.mult, ALU.add))
                link(v.tensor_scalar(lim[:, 2, :], lim[:, 0, :], -1.0, None, ALU.add))
                link(v.tensor_tensor(lim[:, 1, :], lim[:, 1, :], lim[:, 2, :], ALU.min))
                v.tensor_scalar(rng_i[0:1, 0, :], lim[:, 1, :], 0.0, None, ALU.add)
                v.tensor_scalar(rng_i[0:1, 1, :], lim[:, 0, :], 0.0, None, ALU.add).then_inc(ranges_made, 1)
                v.wait_ge(ranges_made, 1)

            v.wait_ge(pool_made, 7)
            for g in range(4):
                a, b = 3 * g, min(3 * g + 3, NT)
                v.wait_ge(x_in[g], 16)
                if g == 3:
                    v.wait_ge(pool_made, 1)
                for t in range(a, b):
                    stats(t)
                v.tensor_scalar(mv[:, a:b, 1], mv[:, a:b, 1], EPS, None, ALU.add).then_inc(var_made, 1)
                v.wait_ge(root_made, g + 1)
                rsqrt(rs[:, a:b], sd[:, a:b], mv[:, a:b, 1], t4[:, 0, a:b], t4[:, 1, a:b])
                for t in range(a, b):
                    if t >= 2:
                        v.wait_ge(xnT_ps, t - 1)
                    v.tensor_scalar(xn[:, t % 2, :], xres[:, t, :], mv[:, t, 0:1], rs[:, t:t + 1],
                                    ALU.subtract, ALU.mult).then_inc(xn_made, 1)
                    if t in PARTS_AT:
                        hot_d_part(PARTS_AT.index(t))
                    elif t == 0:
                        groups_used()
            ranges()

            n_hot = v.alloc_register("v_hot")
            v.reg_mov(n_hot, 0)
            for b in range(NT):
                if b >= 1:
                    v.wait_ge(hot_made, n_hot)
                link(v.scalar_tensor_tensor(src_m[:, :], blk_f[:, :], float(b), src_f[:, :],
                                            ALU.is_equal, ALU.mult))
                first = v.value_load(rng_i[0:1, 0, b:b + 1], min_val=0, max_val=GE - 1)
                last = v.value_load(rng_i[0:1, 1, b:b + 1], min_val=1, max_val=GE)
                with v.Fori(first, last) as i:
                    for j in range(EG):
                        v.reg_add(n_hot, n_hot, 1)
                        v.wait_ge(hot_free, n_hot)
                        v.tensor_scalar(hot_s[:, j, :], iota[:, :],
                                        src_m[:, bass.ds(EG * i + j, 1)], None, ALU.is_equal)\
                         .then_inc(hot_made, 1)

            v.wait_ge(counts_out, NT)
            v.tensor_scalar(t4[:, 3, :], deg[:, :], 1.0, None, ALU.add).then_inc(var_made, 1)
            v.wait_ge(var_made, 5)
            v.wait_ge(root_made, 5)
            rsqrt(dis[:, :], sd[:, :], t4[:, 3, :], t4[:, 0, :], t4[:, 1, :])
            link(v.tensor_reduce(many[:, :], deg[:, :], AX.X, ALU.max))
            v.tensor_scalar(many_b[:, :], many[:, :], 4000.0, None, ALU.is_gt).then_inc(dis_made, 1)
            for t in range(NT):
                if t >= 2:
                    v.wait_ge(disbc_ps, t - 1)
                v.tensor_scalar(xnT[:, t % 2, 0, :], ident[:, :], dis[:, t:t + 1], None, ALU.mult)\
                 .then_inc(diag_made, 1)
            v.wait_ge(many_summed, 1)
            v.tensor_scalar(many_i[0:1, :], bank(5)[0:1, 0:1], 1.0, None, ALU.min).then_inc(many_found, 1)
            v.wait_ge(many_found, 1)
            large = v.value_load(many_i[0:1, 0:1], min_val=0, max_val=1)
            with v.If(large != 0):
                v.wait_ge(ctlo_made, 3 * NT)
                for k in range(NT):
                    v.tensor_tensor(CTx[:, k, :], CT[:, k, :], CTlo[:, k, :], ALU.add).then_inc(whole_made, 1)
            with v.Else():
                v.sem_inc(whole_made, NT)
            v.wait_ge(h_made, NT)
            for t in range(NT):
                v.wait_ge(hhi_made, t + 1)
                v.scalar_tensor_tensor(hlo[:, t, :], h[:, t, :], dis[:, t:t + 1], hhi[:, t, :],
                                       ALU.mult, ALU.subtract).then_inc(hlo_made, 1)
            v.wait_ge(disbc_made, 1)
            n = 0
            for lo, hi in GROUPS:
                for j in range(KD):
                    v.wait_ge(agg1_ps, n + 1)
                    v.tensor_tensor(h1T[:, j, lo:hi], bank(3 + n % 2)[:, 0:hi - lo], dis_bc[:, lo:hi], ALU.mult)\
                     .then_inc(agg1_scaled, 1)
                    n += 1
            for m in range(NT):
                v.wait_ge(h_ps, NT + m + 1)
                v.wait_ge(hhi_made, NT + m + 1)
                v.scalar_tensor_tensor(hlo[:, m, :], bank(5 + m % 2), dis[:, m:m + 1], hhi[:, m, :],
                                       ALU.mult, ALU.subtract).then_inc(hlo_made, 1)
            v.wait_ge(consts_in, 64)
            for t in range(NT):
                f = v.tensor_tensor(xres[:, t, :], xres[:, t, :], b2_bc[:, :], ALU.add)
            link(f)
            v.wait_ge(h_ps, 2 * NT)
            for m in range(NT):
                v.wait_ge(agg2_ps, m + 1)
                f = v.scalar_tensor_tensor(xres[:, m, :], bank(3 + m % 2), dis[:, m:m + 1], xres[:, m, :],
                                           ALU.mult, ALU.add)
                f.then_inc(agg2_out, 1)
                v.wait_ge(agg2_out, m + 1)
                stats(m)
                v.tensor_scalar(mv[:, m, 1:2], mv[:, m, 1:2], EPS, None, ALU.add).then_inc(var_made, 1)
                v.wait_ge(var_made, 6 + m)
                v.wait_ge(root_made, 6 + m)
                rsqrt(rs[:, m:m + 1], sd[:, m:m + 1], mv[:, m, 1:2], t4[:, 0, m:m + 1], t4[:, 1, m:m + 1])
                v.tensor_scalar(xn1[:, m, :], xres[:, m, :], mv[:, m, 0:1], rs[:, m:m + 1],
                                ALU.subtract, ALU.mult).then_inc(xn_made, 1)

            v.wait_ge(lg_ps, NT)
            v.wait_ge(pool_made, 18)
            bc = lambda a: a.unsqueeze(2).to_broadcast([P, NT, EX])
            link(v.tensor_tensor(lg[:, :, :], bank(1)[:, 0:NT * EX].rearrange("p (t e) -> p t e", t=NT),
                                 rb_bc[:, :].unsqueeze(1).to_broadcast([P, NT, EX]), ALU.add))
            for k in range(TOP):
                link(v.tensor_reduce(mx[:, k, :], lg[:, :, :], AX.X, ALU.max))
                link(v.tensor_tensor(sc8[:, 0, :, :], lg[:, :, :], bc(mx[:, k, :]), ALU.is_equal))
                link(v.tensor_tensor(sc8[:, 1, :, :], sc8[:, 0, :, :], iota_e[:, :, :], ALU.mult))
                link(v.tensor_reduce(mx[:, 4, :], sc8[:, 1, :, :], AX.X, ALU.min))
                link(v.tensor_tensor(top[:, k, :, :], iota_e[:, :, :], bc(mx[:, 4, :]), ALU.is_equal))
                if k == 0:
                    v.tensor_scalar(rows[:, :, D + 1], mx[:, 4, :], 0.0, None, ALU.add)
                    link(v.scalar_tensor_tensor(lg[:, :, :], top[:, 0, :, :], -3.0e38, lg[:, :, :],
                                                ALU.mult, ALU.add))
            v.tensor_tensor(mx[:, 2, :], mx[:, 1, :], mx[:, 0, :], ALU.subtract).then_inc(var_made, 1)
            link(v.tensor_tensor(sc8[:, 0, :, :], top[:, 0, :, :], top[:, 1, :, :], ALU.add))
            v.tensor_tensor(mem_b[:, :, :], sc8[:, 0, :, :], bc(valid[:, :]), ALU.mult).then_inc(mem_made, 1)
            v.wait_ge(var_made, 6 + NT)
            v.wait_ge(root_made, 6 + NT)
            link(v.tensor_scalar(mx[:, 4, :], mx[:, 3, :], 1.0, None, ALU.add))
            link(v.reciprocal(wts[:, 0, :], mx[:, 4, :]))
            link(v.tensor_tensor(wts[:, 1, :], wts[:, 0, :], mx[:, 3, :], ALU.mult))
            v.tensor_scalar(rows[:, :, D], token[:, :], 0.0, None, ALU.add)
            v.tensor_scalar(rows[:, :, D + 2], wts[:, 0, :], 0.0, None, ALU.add)
            v.tensor_scalar(rows[:, :, D + 3], wts[:, 1, :], 0.0, None, ALU.add)
            v.wait_ge(rank_ps, 1)
            link(v.tensor_scalar(e8[:, 0, :], bank(5)[:, 0:EX], 1.0, None, ALU.max))
            link(v.tensor_tensor(cmp8[:, :, :], e8[:, 0, :].unsqueeze(2).to_broadcast([P, EX, NT]),
                                 thr[:, :, :], ALU.is_gt))
            link(v.tensor_reduce(e8[:, 1, :], cmp8[:, :, :], AX.X, ALU.add))
            a, b = 1, 2
            for s in (1, 2, 4):
                v.tensor_scalar(e8[:, b, 0:s], e8[:, a, 0:s], 0.0, None, ALU.add)
                link(v.tensor_tensor(e8[:, b, s:EX], e8[:, a, s:EX], e8[:, a, 0:EX - s], ALU.add))
                a, b = b, b + 1
            link(v.tensor_tensor(e8[:, 5, :], e8[:, 4, :], e8[:, 1, :], ALU.subtract))
            v.tensor_scalar(gstart[0:1, 0:EX], e8[0:1, 5, :], 0.0, None, ALU.add)
            v.tensor_scalar(gstart[0:1, EX:EX + 1], e8[0:1, 4, EX - 1:EX], 0.0, None, ALU.add)
            link(v.tensor_scalar(e8[:, 2, :], e8[:, 5, :], float(P), None, ALU.mult))
            link(v.tensor_tensor(rank[:, :, :], bank(2)[:, 0:NT * EX].rearrange("p (t e) -> p t e", t=NT),
                                 e8[:, 2, :].unsqueeze(1).to_broadcast([P, NT, EX]), ALU.add))
            for k in range(TOP):
                link(v.tensor_tensor(sc8[:, 0, :, :], top[:, k, :, :], rank[:, :, :], ALU.mult))
                link(v.tensor_reduce(mx[:, 4, :], sc8[:, 0, :, :], AX.X, ALU.add))
                link(v.tensor_scalar(slots[:, k, :], mx[:, 4, :], 0.0, None, ALU.add))
            v.sem_inc(slots_made, 1)
            link(v.tensor_tensor(sc8[:, 0, :, :], top[:, 0, :, :], bc(wts[:, 0, :]), ALU.mult))
            link(v.tensor_tensor(sc8[:, 1, :, :], top[:, 1, :, :], bc(wts[:, 1, :]), ALU.mult))
            v.tensor_tensor(sc8[:, 0, :, :], sc8[:, 0, :, :], sc8[:, 1, :, :], ALU.add).then_inc(cw_made, 1)
            for t in range(NT):
                v.wait_ge(eb_ps, t + 1)
                v.tensor_tensor(xres[:, t, :], xres[:, t, :], bank((3, 4, 0)[t % 3]), ALU.add).then_inc(agg2_out, 1)


def expert_block(nc, outer, env):
    wall, fc1b, out = env["wall"], env["fc1b"], env["out"]
    ident, raw, gstart, ps = (env[k] for k in ("ident", "raw", "gstart", "ps"))
    raw_in, out_stored, rows_dram = env["raw_in"], env["out_stored"], env["rows_dram"]

    with ExitStack() as ctx:
        def sb(name, shape, dt):
            return ctx.enter_context(nc.sbuf_tensor(name, shape, dt))

        def sem(name):
            return ctx.enter_context(nc.semaphore(name))

        sb("raw_place2", [P, CH, CW], F32)
        whi = sb("whi", [P, CH, KD, D], F32R)
        wlo = sb("wlo", [P, CH, KD, D], F32R)
        bias = sb("bias", [P, 2, 2, D], F32)
        xg = sb("xg", [P, ROW], F32)
        meta = sb("meta", [P, META], F32)
        expert = sb("expert", [P, 1], F32)
        gated = sb("gated", [P, TOP], F32)
        row_w = sb("row_w", [P, 1], F32)
        row_i = sb("row_i", [P, 1], I32)
        xhi = sb("xhi", [P, KD, P], F32R)
        xlo = sb("xlo", [P, KD, P], F32R)
        t1 = sb("t1", [P, 2, D], F32)
        sl = sb("sl", [P, 2, D], F32)
        a = sb("a", [P, 2, D], F32)
        ahi = sb("ahi", [P, 2, KD, P], F32R)
        alo = sb("alo", [P, 2, KD, P], F32R)
        ysb = sb("ysb", [P, D], F32)

        bias_in = sem("bias_in")
        bias_free = sem("bias_free")
        hi_dve = sem("hi_dve")
        hi_act = sem("hi_act")
        lo_dve = sem("lo_dve")
        lo_pool = sem("lo_pool")
        x_loaded = sem("x_loaded")
        xT_ps = sem("xT_ps")
        xhi_made = sem("xhi_made")
        xlo_made = sem("xlo_made")
        fc1_ps = sem("fc1_ps")
        t1_made = sem("t1_made")
        sl_made = sem("sl_made")
        u_made = sem("u_made")
        a_made = sem("a_made")
        aT_ps = sem("aT_ps")
        ahi_made = sem("ahi_made")
        alo_made = sem("alo_made")
        y_ps = sem("y_ps")
        y_out = sem("y_out")
        y_added = sem("y_added")
        rows_set = sem("rows_set")
        expert_set = sem("expert_set")
        meta_used = sem("meta_used")
        meta_kept = sem("meta_kept")
        tick = sem("tick")

        XT, Y = 6, 7
        bank = lambda i: ps[:, i, :]
        chunk = lambda w, c: w[:, c, :, :].rearrange("p k n -> p (k n)")
        x_tiles = rows_dram.rearrange("(g p) d -> g p d", p=P)

        def hi_ready(eng, e, c):
            if c == 0:
                eng.wait_ge(hi_dve, e + 1)
            else:
                eng.wait_ge(hi_act, (CH - 1) * e + ACT_CHUNKS.index(c) + 1)

        def lo_ready(eng, e, c):
            if c < 3:
                eng.wait_ge(lo_dve, 3 * e + c + 1)
            else:
                eng.wait_ge(lo_pool, 3 * e + c - 2)

        def tiles(eng, e):
            first = eng.value_load(gstart[0:1, bass.ds(e, 1)], min_val=0, max_val=MAXT - 1)
            last = eng.value_load(gstart[0:1, bass.ds(e + 1, 1)], min_val=1, max_val=MAXT)
            return first, last

        block = ctx.enter_context(nc.Block())

        @block.sync
        def _(sp):
            def load_bias(e):
                sp.dma_start(bias[:, :, :, :].rearrange("p q g n -> p (q g n)"),
                             fc1b[bass.ds(e, 1), :].rearrange("a n -> (a n)").partition_broadcast(P))\
                  .then_inc(bias_in, 16)

            load_bias(0)
            with sp.Fori(0, EX - 1) as e:
                for c in range(CH):
                    hi_ready(sp, e, c)
                    sp.sem_inc(tick, 1)
                    lo_ready(sp, e, c)
                    sp.sem_inc(tick, 1)
                    sp.dma_start(raw[:, c, :], wall[bass.ds(e * CH + CH + c, 1), :, :]
                                 .rearrange("a p n -> (a p) n")).then_inc(raw_in[c], 16)
                sp.wait_ge(bias_free, e + 1)
                load_bias(e + 1)

        @block.gpsimd
        def _(pool):
            def add_y():
                pool.indirect_dma_start(out, bass.IndirectOffsetOnAxis(row_i[:, :], 0), ysb[:, :], None,
                                        compute_op=ALU.add).then_inc(y_added, 16)

            pool.iota(row_i[:, :], pattern=[[0, 1]], base=N, channel_multiplier=1)
            pool.memset(row_w[:, :], 0.0).then_inc(rows_set, 1)
            pool.wait_ge(rows_set, 1)
            pool.dma_start(ysb[0:1, :], rows_dram[0:1, 0:D]).then_inc(y_added, 16)
            pool.wait_ge(out_stored, 16 * (NT + 1))
            with pool.Fori(0, EX) as e:
                for c in (3, 4, 5):
                    hi_ready(pool, e, c)
                    pool.tensor_tensor(chunk(wlo, c), raw[:, c, :], chunk(whi, c), ALU.subtract)\
                        .then_inc(lo_pool, 1)
                first, last = tiles(pool, e)
                with pool.Fori(first, last) as g:
                    pool.wait_ge(y_out, g + 1)
                    pool.wait_ge(y_added, 16 * g + 16)
                    pool.sem_inc(tick, 1)
                    pool.wait_ge(meta_kept, g + 1)
                    pool.sem_inc(tick, 1)
                    add_y()
            total = pool.value_load(gstart[0:1, EX:EX + 1], min_val=1, max_val=MAXT)
            pool.wait_ge(y_out, total + 1)
            pool.wait_ge(y_added, 16 * total + 16)
            pool.sem_inc(tick, 1)
            pool.wait_ge(meta_kept, total + 1)
            pool.sem_inc(tick, 1)
            add_y()
            pool.wait_ge(y_added, 16 * total + 32)
            pool.sem_inc(tick, 1)

        @block.tensor
        def _(pe):
            def transposes(to, of):
                for k in range(KD):
                    tr = pe.transpose(to[:, k * P:(k + 1) * P], of[:, k * P:(k + 1) * P], ident[:, :])
                return tr

            pe.wait_ge(x_loaded, 16)
            transposes(bank(Y), xg).then_inc(y_ps, 1)
            transposes(bank(XT), xg).then_inc(xT_ps, 1)
            pe.sem_inc(fc1_ps, 1)

            def product(o, hi, lo, c, e=None, part=(0, 3 * KD), start=True, stop=True):
                steps = [(k, l, w) for l, w in ((hi, whi), (lo, whi), (hi, wlo)) for k in range(KD)]
                for n in range(*part):
                    if n == 0:
                        hi_ready(pe, e, c)
                    if n == 2 * KD:
                        lo_ready(pe, e, c)
                    k, l, w = steps[n]
                    mm = pe.matmul(o, l[:, k, :], w[:, c, k, :], start=start and n == 0,
                                   stop=stop and n == len(steps) - 1)
                return mm

            with pe.Fori(0, EX) as e:
                first, last = tiles(pe, e)
                with pe.Fori(first, last) as g:
                    def turn(q):
                        pe.wait_ge(a_made, 2 * g + q + 1)
                        transposes(bank(4 + q), a[:, q, :]).then_inc(aT_ps, 1)

                    pe.wait_ge(xhi_made, g + 1)
                    product(bank(0), xhi, xlo, 0, e, (0, KD), stop=False)
                    pe.wait_ge(xlo_made, g + 1)
                    product(bank(0), xhi, xlo, 0, e, (KD, 3 * KD)).then_inc(fc1_ps, 1)
                    for c in (1, 2):
                        product(bank(c), xhi, xlo, c, e).then_inc(fc1_ps, 1)
                    product(bank(3), xhi, xlo, 3, e, (0, KD), stop=False)
                    turn(0)
                    product(bank(3), xhi, xlo, 3, e, (KD, 3 * KD)).then_inc(fc1_ps, 1)
                    pe.wait_ge(ahi_made, 2 * g + 1)
                    pe.wait_ge(alo_made, 2 * g + 1)
                    pe.wait_ge(y_out, g + 1)
                    product(bank(Y), ahi[:, 0, :, :], alo[:, 0, :, :], 4, e, (0, 7), stop=False)
                    turn(1)
                    product(bank(Y), ahi[:, 0, :, :], alo[:, 0, :, :], 4, e, (7, 3 * KD), stop=False)
                    pe.wait_ge(x_loaded, 16 * g + 32)
                    transposes(bank(XT), xg).then_inc(xT_ps, 1)
                    pe.wait_ge(ahi_made, 2 * g + 2)
                    product(bank(Y), ahi[:, 1, :, :], alo[:, 1, :, :], 5, e, (0, KD), start=False, stop=False)
                    pe.wait_ge(alo_made, 2 * g + 2)
                    product(bank(Y), ahi[:, 1, :, :], alo[:, 1, :, :], 5, e, (KD, 3 * KD), start=False)\
                        .then_inc(y_ps, 1)

        @block.scalar
        def _(act):
            def load_x(g):
                act.wait_ge(meta_kept, g)
                act.dma_start(xg[:, :], x_tiles[bass.ds(g, 1), :, :].rearrange("a p d -> (a p) d"))\
                   .then_inc(x_loaded, 16)

            def weigh_y(g):
                act.wait_ge(y_added, 16 * g + 16)
                act.wait_ge(meta_kept, g + 1)
                act.wait_ge(y_ps, g + 1)
                act.activation(ysb[:, :], bank(Y), ACT.Copy, scale=row_w[:, :]).then_inc(y_out, 1)

            def copy_x(n):
                act.wait_ge(xT_ps, n)
                act.activation(xhi[:, :, :].rearrange("p k n -> p (k n)"), bank(XT), ACT.Copy)\
                   .then_inc(xhi_made, 1)

            act.dma_start(xg[:, :], x_tiles[0, :, :]).then_inc(x_loaded, 16)
            copy_x(1)
            act.wait_ge(rows_set, 1)
            act.preload_act_table(ACT.Silu)
            with act.Fori(0, EX) as e:
                for c in ACT_CHUNKS:
                    if c == 4:
                        first, last = tiles(act, e)
                        act.wait_ge(y_ps, first + 1)
                    act.wait_ge(raw_in[c], 16 * e + 16)
                    act.activation(chunk(whi, c), raw[:, c, :], ACT.Copy).then_inc(hi_act, 1)
                with act.Fori(first, last) as g:
                    act.wait_ge(xT_ps, g + 1)
                    load_x(g + 1)
                    weigh_y(g)
                    for q in range(2):
                        act.wait_ge(t1_made, 2 * g + q + 1)
                        act.activation(sl[:, q, :], t1[:, q, :], ACT.Silu).then_inc(sl_made, 1)
                        act.wait_ge(aT_ps, 2 * g + q + 1)
                        act.activation(ahi[:, q, :, :].rearrange("p k n -> p (k n)"), bank(4 + q), ACT.Copy)\
                           .then_inc(ahi_made, 1)
                    copy_x(g + 2)
            total = act.value_load(gstart[0:1, EX:EX + 1], min_val=1, max_val=MAXT)
            weigh_y(total)

        @block.vector
        def _(v):
            def lower_x(n):
                v.wait_ge(xhi_made, n)
                v.tensor_tensor(xlo[:, :, :].rearrange("p k n -> p (k n)"), bank(XT),
                                xhi[:, :, :].rearrange("p k n -> p (k n)"), ALU.subtract).then_inc(xlo_made, 1)

            def keep_meta():
                v.tensor_copy(meta[:, :], xg[:, D:ROW]).then_inc(meta_kept, 1)

            v.memset(expert[:, :], float(-EX)).then_inc(expert_set, 1)
            v.wait_ge(expert_set, 1)
            v.wait_ge(x_loaded, 16)
            keep_meta()
            lower_x(1)
            with v.Fori(0, EX) as e:
                v.wait_ge(raw_in[0], 16 * e + 16)
                v.tensor_copy(chunk(whi, 0), raw[:, 0, :]).then_inc(hi_dve, 1)
                for c in range(3):
                    if c == 2:
                        v.wait_ge(bias_in, 16 * e + 16)
                    hi_ready(v, e, c)
                    v.tensor_tensor(chunk(wlo, c), raw[:, c, :], chunk(whi, c), ALU.subtract).then_inc(lo_dve, 1)
                first, last = tiles(v, e)
                with v.Fori(first, last) as g:
                    def gate(q):
                        v.wait_ge(fc1_ps, 4 * g + 2 * q + 2)
                        v.tensor_tensor(t1[:, q, :], bank(2 * q), bias[:, q, 0, :], ALU.add).then_inc(t1_made, 1)

                    def up(q):
                        v.wait_ge(fc1_ps, 4 * g + 2 * q + 3)
                        v.tensor_tensor(a[:, q, :], bank(2 * q + 1), bias[:, q, 1, :], ALU.add)\
                         .then_inc(u_made, 1)
                        v.wait_ge(u_made, 2 * g + q + 1)
                        v.wait_ge(sl_made, 2 * g + q + 1)
                        v.tensor_tensor(a[:, q, :], a[:, q, :], sl[:, q, :], ALU.mult).then_inc(a_made, 1)

                    def lower_a(q):
                        v.wait_ge(ahi_made, 2 * g + q + 1)
                        v.tensor_tensor(alo[:, q, :, :].rearrange("p k n -> p (k n)"), bank(4 + q),
                                        ahi[:, q, :, :].rearrange("p k n -> p (k n)"), ALU.subtract)\
                         .then_inc(alo_made, 1)

                    gate(0)
                    up(0)
                    gate(1)
                    lower_a(0)
                    up(1)
                    lower_a(1)
                    lower_x(g + 2)
                    v.wait_ge(y_added, 16 * g + 32)
                    v.tensor_scalar(row_i[:, :], meta[:, 0:1], 0.0, None, ALU.add).then_inc(meta_used, 1)
                    v.scalar_tensor_tensor(gated[:, 0:1], meta[:, 1:2], expert[:, :], meta[:, 2:3],
                                           ALU.is_equal, ALU.mult).then_inc(meta_used, 1)
                    v.scalar_tensor_tensor(gated[:, 1:2], meta[:, 1:2], expert[:, :], meta[:, 3:4],
                                           ALU.not_equal, ALU.mult).then_inc(meta_used, 1)
                    v.wait_ge(meta_used, 3 * g + 3)
                    v.tensor_tensor(row_w[:, :], gated[:, 0:1], gated[:, 1:2], ALU.add)
                    keep_meta()
                v.sem_inc(bias_free, 1)
                v.tensor_scalar(expert[:, :], expert[:, :], 1.0, None, ALU.add).then_inc(expert_set, 1)
                v.wait_ge(expert_set, e + 2)


def kernel(**inputs):
    import numpy as np
    import concourse.bacc as bacc
    from concourse.bass_utils import run_bass_kernel_spmd

    arr = {k: np.asarray(v) for k, v in inputs.items()}

    def edges(a, pad):
        whole = np.full(ET * P, pad, np.int32)
        whole[:EDGES] = a
        return np.ascontiguousarray(whole.reshape(ET, P).T)

    fc1 = arr["L0_ffn_fc1_w"].reshape(EX, 2, 2, D, KD, P).transpose(0, 2, 1, 5, 4, 3).reshape(EX, 4, P, CW)
    fc2 = arr["L0_ffn_fc2_w"].reshape(EX, D, 2, KD, P).transpose(0, 2, 4, 3, 1).reshape(EX, 2, P, CW)
    arrays = {
        "x": arr["x"],
        "src": edges(arr["src"], 0),
        "dst": edges(arr["dst"], NO_NODE),
        "W1": arr["L0_gnn_W1"],
        "b1": np.ascontiguousarray(arr["L0_gnn_b1"].reshape(KD, P).T),
        "W2": arr["L0_gnn_W2"],
        "b2": arr["L0_gnn_b2"],
        "rw": np.ascontiguousarray(arr["L0_ffn_router_w"].T),
        "rb": arr["L0_ffn_router_b"],
        "wall": np.ascontiguousarray(np.concatenate([fc1, fc2], axis=1).reshape(EX * CH, P, CW)),
        "fc1b": np.ascontiguousarray(
            arr["L0_ffn_fc1_b"].reshape(EX, 2, 2, D).transpose(0, 2, 1, 3).reshape(EX, 4 * D)),
        "fc2b": arr["L0_ffn_fc2_b"],
    }
    nc = bacc.Bacc("TRN2", target_bir_lowering=False, num_devices=1)
    args = [nc.dram_tensor(f"in_{k}", a.shape, mybir.dt.from_np(a.dtype), kind="ExternalInput").ap()
            for k, a in arrays.items()]
    out = nc.dram_tensor("out", (N + P, D), F32, kind="ExternalOutput").ap()
    build(nc, *args, out)
    r = run_bass_kernel_spmd(nc, [{f"in_{k}": a for k, a in arrays.items()}], core_ids=[0])
    return r.results[0]["out"][:N]
```

```python
from contextlib import ExitStack

import concourse.bass as bass
from concourse import mybir

F32 = mybir.dt.float32
F32R = mybir.dt.float32r
BF16 = mybir.dt.bfloat16
FP8 = mybir.dt.float8e4
FP16 = mybir.dt.float16
I32 = mybir.dt.int32
ALU = mybir.AluOpType
ACT = mybir.ActivationFunctionType
AX = mybir.AxisListType

P = 128
N = 1250
D = 512
EDGES = 20000
NT = -(-N // P)
NP = NT * P
TAIL = N - (NT - 1) * P
EG = 3
GE = -(-EDGES // (EG * P))
ET = EG * GE
KD = D // P
EX = 8
TOP = 2
HID = 1024
CH = 3 * HID // D
PARTS_AT = (1, 3, 4, 6, 7, 8, 9)
ACT_CHUNKS = (3, 2, 4, 5)
CW = KD * D
MAXT = (TOP * N + (P - 1) * EX + EX) // P
GT = MAXT + 2
EPS = 1e-5
NO_NODE = 4095


def build(nc, x, src, dst, W1, b1, W2, b2, rw, rb, wall, fc1b, fc2b, out):
    rows_dram = nc.dram_tensor("expert_inputs", (N + P, D), F32).ap()

    with ExitStack() as ctx:
        def sb(name, shape, dt, c=ctx):
            return c.enter_context(nc.sbuf_tensor(name, shape, dt))

        def sem(name):
            return ctx.enter_context(nc.semaphore(name))

        ps = ctx.enter_context(nc.psum_tensor("ps", [P, 8, 512], F32))
        ident = sb("ident", [P, P], F32)
        xres = sb("xres", [P, NT, D], F32)
        tok_i = sb("tok_i", [P, GT], I32)
        tok_w = sb("tok_w", [P, GT], F32)
        xg = sb("xg", [P, D], F32)
        next_i = sb("next_i", [P, 1], I32)
        gstart = sb("gstart", [1, EX + 1], I32)

        with nc.sbuf_tensor("raw", [P, CH, CW], F32) as raw:
            pass

        raw_in = [sem(f"raw_in{c}") for c in range(CH)]
        rows_stored = sem("rows_stored")
        next_set = sem("next_set")
        x_loaded = sem("x_loaded")
        out_stored = sem("out_stored")
        graph_block(nc, ctx, locals())
        expert_block(nc, ctx, locals())


def graph_block(nc, outer, env):
    x, src, dst, W1, b1, W2, b2, rw, rb, wall, fc2b, out = (env[k] for k in (
        "x", "src", "dst", "W1", "b1", "W2", "b2", "rw", "rb", "wall", "fc2b", "out"))
    ident, xres, raw, tok_i, tok_w, xg, next_i, gstart, ps = (env[k] for k in (
        "ident", "xres", "raw", "tok_i", "tok_w", "xg", "next_i", "gstart", "ps"))
    raw_in, rows_stored, next_set, x_loaded, out_stored, rows_dram = (env[k] for k in (
        "raw_in", "rows_stored", "next_set", "x_loaded", "out_stored", "rows_dram"))

    with ExitStack() as ctx:
        def sb(name, shape, dt):
            return ctx.enter_context(nc.sbuf_tensor(name, shape, dt))

        def sem(name):
            return ctx.enter_context(nc.semaphore(name))

        with (nc.sbuf_tensor("hot_d", [P, ET, P], BF16) as hot_d,
              nc.sbuf_tensor("flags", [P, NT * ET], BF16) as flags):
            pass
        with (nc.sbuf_tensor("hhi", [P, NT, D], F32R) as hhi,
              nc.sbuf_tensor("hlo", [P, NT, D], F32R) as hlo,
              nc.sbuf_tensor("dis_bc", [P, NP], F32) as dis_bc):
            pass
        sb("raw_place", [P, CH, CW], F32)
        with nc.sbuf_tensor("CTx", [P, NT, NP], F32) as CTx:
            pass
        CT = sb("CT", [P, NT, NP], F32R)
        CTlo = sb("CTlo", [P, NT, NP], FP8)
        with (nc.sbuf_tensor("cwT", [3 * EX, NT, P], F32R) as cwT,
              nc.sbuf_tensor("fc2b_sb", [3 * EX, D], F32) as fc2b_sb,
              nc.sbuf_tensor("fc2b_hi", [3 * EX, D], F32R) as fc2b_hi,
              nc.sbuf_tensor("fc2b_lo", [3 * EX, D], F32) as fc2b_lo,
              nc.sbuf_tensor("fc2b_3", [3 * EX, D], F32R) as fc2b_3):
            pass
        with nc.sbuf_tensor("h1hi", [P, KD, NP], F32R) as h1hi:
            pass
        h = sb("h", [P, NT, D], F32)
        with (nc.sbuf_tensor("hot_s", [P, EG, NP], BF16) as hot_s,
              nc.sbuf_tensor("eyez", [P, 2 * NP], BF16) as eyez,
              nc.sbuf_tensor("iota", [P, NP], FP16) as iota,
              nc.sbuf_tensor("src_i", [P, ET], I32) as src_i,
              nc.sbuf_tensor("dst_i", [P, ET], I32) as dst_i):
            pass
        with nc.sbuf_tensor("ranges_row", [1, 2 * NP], F32) as spare:
            pass
        with nc.sbuf_tensor("h1lo", [P, KD, NP], F32R) as h1lo:
            pass
        h1T = sb("h1T", [P, KD, NP], F32)
        xn1 = h1T[:, :, :].rearrange("p a b -> p (a b)").rearrange("p (t d) -> p t d", t=NT)
        wts = sb("wts", [P, TOP, NT], F32)
        slot = sb("slot", [P, TOP, NT], I32)
        part_i = sb("part_i", [P, 2, TOP, NT], I32)
        part_f = sb("part_f", [P, 2, TOP, NT], F32)
        token = sb("token", [P, NT], F32)
        iota_g = sb("iota_g", [P, NT, GT], F32)
        pad_row = sb("pad_row", [P, 1], F32)
        ct_flat = CTx[:, :, :].rearrange("p k n -> p (k n)")
        at_place = ct_flat[:, 0:TOP * NT * P].rearrange("p (k t n) -> p k t n", k=TOP, t=NT)
        in_tile = ct_flat[:, TOP * NT * P:TOP * NT * (P + 3 * GT)].rearrange(
            "p (k t q g) -> p k t q g", k=TOP, t=NT, q=3)
        cw = sb("cw", [P, NT, EX], F32)
        cw3 = sb("cw3", [P, NT, 3, EX], F32)
        in_hi = sb("in_hi", [P, 2], F32)
        id_w = sb("id_w", [P, 2, GT], F32)
        with nc.sbuf_tensor("Wlo", [P, KD, D], F32R) as Wlo:
            pass
        Wg = sb("Wg", [P, KD, D], F32)
        with nc.sbuf_tensor("Whi", [P, KD, D], F32R) as Whi:
            pass
        Cs = sb("Cs", [P, NP], F32)
        xn = sb("xn", [P, 2, D], F32)
        xnT = sb("xnT", [P, 2, KD, P], F32)
        diag = xnT[:, :, :, :].rearrange("p a k n -> p (a k) n")
        b2_bc = sb("b2_bc", [P, D], F32)
        src_f = sb("src_f", [P, ET], F32)
        dst_f = sb("dst_f", [P, ET], FP16)
        blk_f = sb("blk_f", [P, ET], F32)
        src_m = sb("src_m", [P, ET], F32)
        many = sb("many", [P, 1], F32)
        many_b = sb("many_b", [P, 1], BF16)
        many_i = sb("many_i", [1, 1], I32)
        b1c = sb("b1c", [P, KD], F32)
        rwT = sb("rwT", [P, KD, EX], F32)
        rb_bc = sb("rb_bc", [P, EX], F32)
        stat = sb("stat", [P, 6], F32)
        mv = sb("mv", [P, NT, 2], F32)
        sd = sb("sd", [P, NT], F32)
        rs = sb("rs", [P, NT], F32)
        deg = sb("deg", [P, NT], F32)
        dis = sb("dis", [P, NT], F32)
        t4 = sb("t4", [P, 4, NT], F32)
        ones_b = sb("ones_b", [P, P], BF16)
        ones_f = sb("ones_f", [P, P], F32)
        iota_p = sb("iota_p", [P, P], F32)
        below = sb("below", [P, P], BF16)
        lg = sb("lg", [P, NT, EX], F32)
        valid = sb("valid", [P, NT], F32)
        iota_e = sb("iota_e", [P, NT, EX], F32)
        sc8 = sb("sc8", [P, 2, NT, EX], F32)
        top = sb("top", [P, TOP, NT, EX], F32)
        mx = sb("mx", [P, 6, NT], F32)
        mem_b = sb("mem_b", [P, NT, EX], BF16)
        rank = sb("rank", [P, NT, EX], F32)
        e8 = sb("e8", [P, 6, EX], F32)
        thr = sb("thr", [P, EX, NT], F32)
        cmp8 = sb("cmp8", [P, EX, NT], F32)
        rng_i = sb("rng_i", [1, 2, NT], I32)

        edges_in = sem("edges_in")
        x_in = [sem(f"x_in{i}") for i in range(4)]
        w1_in = sem("w1_in")
        w2_in = sem("w2_in")
        consts_in = sem("consts_in")
        fc2b_in = sem("fc2b_in")
        fc2b_split = sem("fc2b_split")
        zero_out = sem("zero_out")
        pool_made = sem("pool_made")
        flags_made = sem("flags_made")
        flags_summed = sem("flags_summed")
        ranges_made = sem("ranges_made")
        dve = sem("dve")
        var_made = sem("var_made")
        root_made = sem("root_made")
        xn_made = sem("xn_made")
        xnT_ps = sem("xnT_ps")
        xnT_made = sem("xnT_made")
        h_ps = sem("h_ps")
        h_made = sem("h_made")
        hot_d_made = sem("hot_d_made")
        hot_made = sem("hot_made")
        hot_free = sem("hot_free")
        counts_ps = sem("counts_ps")
        counts_out = sem("counts_out")
        ct_ps = sem("ct_ps")
        ct_made = sem("ct_made")
        ct_copied = sem("ct_copied")
        ctlo_made = sem("ctlo_made")
        whole_made = sem("whole_made")
        diag_made = sem("diag_made")
        disbc_ps = sem("disbc_ps")
        disbc_made = sem("disbc_made")
        dis_made = sem("dis_made")
        many_summed = sem("many_summed")
        many_found = sem("many_found")
        hhi_made = sem("hhi_made")
        hlo_made = sem("hlo_made")
        agg1_ps = sem("agg1_ps")
        agg1_scaled = sem("agg1_scaled")
        h1T_made = sem("h1T_made")
        h1hi_made = sem("h1hi_made")
        h1lo_made = sem("h1lo_made")
        w2hi_made = sem("w2hi_made")
        w2lo_made = sem("w2lo_made")
        agg2_ps = sem("agg2_ps")
        agg2_out = sem("agg2_out")
        lg_ps = sem("lg_ps")
        mem_made = sem("mem_made")
        rank_ps = sem("rank_ps")
        spots_made = sem("spots_made")
        table_ps = sem("table_ps")
        cw_made = sem("cw_made")
        cwT_ps = sem("cwT_ps")
        cwT_made = sem("cwT_made")
        eb_ps = sem("eb_ps")

        BIAS_BANKS = (3, 4, 0)
        GROUPS = [(0, 512), (512, 1024), (1024, NP)]
        bank = lambda i: ps[:, i, :]
        flat = ps[:, :, :].rearrange("p b n -> p (b n)")

        block = ctx.enter_context(nc.Block())

        @block.sync
        def _(sp):
            sp.dma_start(dst_i[:, :], dst).then_inc(edges_in, 16)
            sp.dma_start(src_i[:, :], src).then_inc(edges_in, 16)
            xt = x[0:(NT - 1) * P, :].rearrange("(t p) d -> p t d", p=P)
            for i in range(3):
                sp.dma_start(xres[:, 3 * i:3 * i + 3, :], xt[:, 3 * i:3 * i + 3, :]).then_inc(x_in[i], 16)
            sp.dma_start(Wg[:, :, :], W1.rearrange("(k p) n -> p k n", p=P)).then_inc(w1_in, 16)
            sp.wait_ge(pool_made, 1)
            sp.dma_start(xres[0:TAIL, NT - 1, :], x[(NT - 1) * P:N, :]).then_inc(x_in[3], 16)
            sp.dma_start(b1c[:, :], b1).then_inc(consts_in, 16)
            sp.dma_start(rwT[:, :, :], rw.rearrange("(k p) e -> p k e", p=P)).then_inc(consts_in, 16)
            sp.dma_start(rb_bc[:, :], rb.partition_broadcast(P)).then_inc(consts_in, 16)
            sp.dma_start(b2_bc[:, :], b2.partition_broadcast(P)).then_inc(consts_in, 16)
            sp.wait_ge(pool_made, 3)
            zeros = eyez[:, 0:2 * D].bitcast(F32)
            sp.dma_start(rows_dram[N:N + P, :], zeros).then_inc(zero_out, 16)
            sp.dma_start(out[N:N + P, :], zeros).then_inc(zero_out, 16)
            sp.wait_ge(h_ps, NT)
            sp.dma_start(Wg[:, :, :], W2.rearrange("(k p) n -> p k n", p=P)).then_inc(w2_in, 16)
            sp.wait_ge(h_ps, 2 * NT)
            for i in range(3):
                sp.dma_start(fc2b_sb[i * EX:(i + 1) * EX, :], fc2b).then_inc(fc2b_in, 16)
            for t in range(NT):
                n = P if t < NT - 1 else TAIL
                sp.wait_ge(xn_made, NT + t + 1)
                sp.dma_start(rows_dram[t * P:t * P + n, :], xn1[0:n, t, :]).then_inc(rows_stored, 16)
            sp.wait_ge(agg2_ps, NT)
            for c in range(CH):
                sp.dma_start(raw[:, c, :], wall[c, :, :]).then_inc(raw_in[c], 16)
            sp.wait_ge(rows_stored, 16 * NT)
            for t in range(NT):
                n = P if t < NT - 1 else TAIL
                sp.wait_ge(agg2_out, NT + t + 1)
                sp.dma_start(out[t * P:t * P + n, :], xres[0:n, t, :]).then_inc(out_stored, 16)

        @block.gpsimd
        def _(pool):
            made = 0

            def step(ins):
                nonlocal made
                made += 1
                ins.then_inc(pool_made, 1)
                pool.wait_ge(pool_made, made)

            step(pool.memset(xres[:, NT - 1, :], 0.0))
            step(pool.memset(eyez[:, :], 0.0))
            mid = eyez[:, NP - P:NP]
            step(pool.affine_select(out=mid, in_=mid, compare_op=ALU.not_equal, fill=1.0, base=0,
                                    pattern=[[-1, P]], channel_multiplier=1))
            step(pool.memset(ident[:, :], 0.0))
            step(pool.affine_select(out=ident[:, :], in_=ident[:, :], compare_op=ALU.not_equal, fill=1.0,
                                    base=0, pattern=[[-1, P]], channel_multiplier=1))
            step(pool.memset(ones_b[:, :], 1.0))
            step(pool.iota(iota[:, :], pattern=[[1, NP]], base=1, channel_multiplier=0,
                           allow_small_or_imprecise_dtypes=True))
            step(pool.iota(spare[0:1, 0:GE], pattern=[[1, GE]], base=1, channel_multiplier=0,
                           allow_small_or_imprecise_dtypes=True))
            step(pool.iota(spare[0:1, GE:2 * GE], pattern=[[-1, GE]], base=GE, channel_multiplier=0,
                           allow_small_or_imprecise_dtypes=True))
            step(pool.memset(ones_f[:, :], 1.0))
            step(pool.affine_select(out=below[:, :], in_=ones_b[:, :], compare_op=ALU.is_gt, fill=0.0,
                                    base=0, pattern=[[1, P]], channel_multiplier=-1))
            step(pool.memset(valid[:, :], 1.0))
            step(pool.affine_select(out=valid[:, :], in_=valid[:, :], compare_op=ALU.is_gt, fill=0.0,
                                    base=N, pattern=[[-P, NT]], channel_multiplier=-1))
            step(pool.iota(iota_e[:, :, :], pattern=[[0, NT], [1, EX]], base=-EX, channel_multiplier=0,
                           allow_small_or_imprecise_dtypes=True))
            step(pool.iota(thr[:, :, :], pattern=[[0, EX], [P, NT]], base=0, channel_multiplier=0,
                           allow_small_or_imprecise_dtypes=True))
            step(pool.iota(token[:, :], pattern=[[P, NT]], base=1, channel_multiplier=1,
                           allow_small_or_imprecise_dtypes=True))
            step(pool.iota(iota_g[:, :, :], pattern=[[0, NT], [1, GT]], base=0, channel_multiplier=0,
                           allow_small_or_imprecise_dtypes=True))
            step(pool.iota(iota_p[:, :], pattern=[[1, P]], base=1, channel_multiplier=0,
                           allow_small_or_imprecise_dtypes=True))
            step(pool.iota(pad_row[:, :], pattern=[[0, 1]], base=N + 1, channel_multiplier=1,
                           allow_small_or_imprecise_dtypes=True))
            for n in range(3 * NT):
                b, q = n // 3, n % 3
                m = min(4, NT - 4 * q)
                pool.wait_ge(ct_copied, n + 1)
                pool.wait_ge(ct_made, n + 1)
                pool.tensor_tensor(CTlo[:, 4 * q:4 * q + m, b * P:(b + 1) * P],
                                   xn[:, n % 2, 0:m * P].rearrange("p (k n) -> p k n", k=m),
                                   CT[:, 4 * q:4 * q + m, b * P:(b + 1) * P], ALU.subtract, saturate=False)\
                    .then_inc(ctlo_made, 1)
            pool.wait_ge(rows_stored, 16 * NT)
            pool.wait_ge(next_set, 1)
            pool.indirect_dma_start(xg[:, :], None, rows_dram,
                                    bass.IndirectOffsetOnAxis(next_i[:, :], 0)).then_inc(x_loaded, 16)

        @block.tensor
        def _(pe):
            pe.wait_ge(flags_made, 1)
            pe.wait_ge(pool_made, 6)
            for a in range(0, NT * ET, 512):
                b = min(a + 512, NT * ET)
                mm = pe.matmul(flat[0:1, a:b], ones_b[:, 0:1], flags[:, a:b], start=True, stop=True)
            mm.then_inc(flags_summed, 1)

            def either(large, products):
                with pe.If(large != 0):
                    pe.wait_ge(whole_made, NT)
                    products(CTx, lambda part: part.bitcast(F32))
                with pe.Else():
                    products(CT, lambda part: part)

            def transposes(t, of, to):
                for k in range(KD):
                    tr = pe.transpose(to[:, k * P:(k + 1) * P], of[:, k * P:(k + 1) * P], ident[:, :])
                return tr

            for t in range(NT + 1):
                if t < NT:
                    pe.wait_ge(xn_made, t + 1)
                    if t >= 2:
                        pe.wait_ge(xnT_made, t - 1)
                    transposes(t, xn[:, t % 2, :], bank(6 + t % 2)).then_inc(xnT_ps, 1)
                if t >= 1:
                    s = t - 1
                    if s == 0:
                        pe.wait_ge(w1_in, 16)
                    pe.wait_ge(xnT_made, s + 1)
                    if s >= 2:
                        pe.wait_ge(h_made, s - 1)
                    for k in range(KD):
                        mm = pe.matmul(bank(4 + s % 2), xnT[:, s % 2, k, :], Wg[:, k, :],
                                       start=(k == 0), stop=(k == KD - 1))
                    mm.then_inc(h_ps, 1)

            n_hot = pe.alloc_register("pe_hot")
            pe.reg_mov(n_hot, 0)
            pe.wait_ge(ranges_made, 1)
            pe.wait_ge(hot_d_made, len(PARTS_AT))
            pe.sem_inc(hot_free, EG)

            def ct_block(b, parts):
                for q in parts:
                    if q == 0:
                        pe.wait_ge(counts_out, b + 1)
                    n = 3 * b + q
                    if n >= 2:
                        pe.wait_ge(ct_made, n - 1)
                    for k in range(4 * q, min(4 * q + 4, NT)):
                        tr = pe.transpose(bank(6 + n % 2)[:, (k % 4) * P:(k % 4 + 1) * P],
                                          Cs[:, k * P:(k + 1) * P], ident[:, :])
                    tr.then_inc(ct_ps, 1)

            for b in range(NT):
                first = pe.value_load(rng_i[0:1, 0, b:b + 1], min_val=0, max_val=GE - 1)
                last = pe.value_load(rng_i[0:1, 1, b:b + 1], min_val=1, max_val=GE)
                o = flat[:, 1536 * (b % 2):1536 * (b % 2) + NP + 1]
                if b == 1:
                    pe.wait_ge(h_made, NT)
                if b >= 2:
                    pe.wait_ge(counts_out, b - 1)
                at = NP - P - b * P
                for lo, hi in ((0, 512), (512, 1024), (1024, NP + 1)):
                    pe.matmul(o[:, lo:hi], eyez[:, NP - P:NP], eyez[:, at + lo:at + hi],
                              start=True, stop=False, skip_group_check=True)
                if b >= 2:
                    ct_block(b - 2, (2,))
                with pe.Fori(first, last) as i:
                    for j in range(EG):
                        pe.reg_add(n_hot, n_hot, 1)
                        pe.wait_ge(hot_made, n_hot)
                        to_tile = hot_d[:, bass.ds(EG * i + j, 1), :].rearrange("p a n -> p (a n)")
                        source = hot_s[:, j, :]
                        for lo, hi in GROUPS:
                            pe.matmul(o[:, lo:hi], to_tile, source[:, lo:hi],
                                      start=False, stop=False, skip_group_check=True)
                        pe.matmul(o[:, NP:NP + 1], to_tile, flags[:, bass.ds(EG * i + (b * ET + j), 1)],
                                  start=False, stop=False, skip_group_check=True).then_inc(hot_free, 1)
                pe.matmul(o[:, 0:1], eyez[:, NP - P:NP], eyez[:, 0:1], start=False, stop=True,
                          skip_group_check=True).then_inc(counts_ps, 1)
                if b >= 1:
                    ct_block(b - 1, (0, 1))
            ct_block(NT - 2, (2,))
            ct_block(NT - 1, (0, 1, 2))

            pe.wait_ge(dis_made, 1)
            pe.matmul(bank(5)[0:1, 0:1], many_b[:, :], ones_b[:, 0:1], start=True, stop=True)\
              .then_inc(many_summed, 1)
            pe.wait_ge(pool_made, 10)

            def spread_dis():
                for t in range(NT):
                    pe.wait_ge(diag_made, t + 1)
                    pe.matmul(flat[:, t * P:(t + 1) * P], ones_f[:, :], diag[:, t % 8, :],
                              start=(t % 4 == 0), stop=True, skip_group_check=True).then_inc(disbc_ps, 1)

            pe.wait_ge(ct_made, 3 * NT)
            pe.wait_ge(many_found, 1)
            large = pe.value_load(many_i[0:1, 0:1], min_val=0, max_val=1)

            def aggregate1(counts, view):
                n = 0
                for lo, hi in GROUPS:
                    for j in range(KD):
                        if n >= 2:
                            pe.wait_ge(agg1_scaled, n - 1)
                        for i in range(2 * NT):
                            k, part = i % NT, (hhi, hlo)[i // NT]
                            if n == 0:
                                pe.wait_ge((hhi_made, hlo_made)[i // NT], k + 1)
                            mm = pe.matmul(bank(3 + n % 2)[:, 0:hi - lo], view(part[:, k, j * P:(j + 1) * P]),
                                           counts[:, k, lo:hi], start=(i == 0), stop=(i == 2 * NT - 1))
                        mm.then_inc(agg1_ps, 1)
                        if n == 0:
                            spread_dis()
                        n += 1

            either(large, aggregate1)
            pe.wait_ge(w2hi_made, 1)
            pe.wait_ge(w2lo_made, 1)
            for m in range(NT):
                pe.wait_ge(h1lo_made, KD * (m // 4 + 1))
                if m >= 2:
                    pe.wait_ge(hhi_made, NT + m - 1)
                    pe.wait_ge(hlo_made, NT + m - 1)
                for i, (l, w) in enumerate(((h1hi, Whi), (h1lo, Whi), (h1hi, Wlo))):
                    for k in range(KD):
                        mm = pe.matmul(bank(5 + m % 2), l[:, k, m * P:(m + 1) * P], w[:, k, :],
                                       start=(i == 0 and k == 0), stop=(i == 2 and k == KD - 1))
                mm.then_inc(h_ps, 1)
            pe.wait_ge(disbc_made, 1)

            def aggregate2(counts, view):
                for m in range(NT + 3):
                    if m < NT:
                        if m >= 2:
                            pe.wait_ge(agg2_out, m - 1)
                        for i in range(2 * NT):
                            k, part = i % NT, (hhi, hlo)[i // NT]
                            if m == 0:
                                pe.wait_ge((hhi_made, hlo_made)[i // NT], NT + k + 1)
                            mm = pe.matmul(bank(3 + m % 2), counts[:, k, m * P:(m + 1) * P],
                                           view(part[:, k, :]), start=(i == 0), stop=(i == 2 * NT - 1))
                        mm.then_inc(agg2_ps, 1)
                    if 2 <= m <= NT + 1:
                        s = m - 2
                        pe.wait_ge(xn_made, NT + s + 1)
                        transposes(s, xn1[:, s, :], bank(6 + s % 2)).then_inc(xnT_ps, 1)
                    if m >= 3:
                        s = m - 3
                        pe.wait_ge(xnT_made, NT + s + 1)
                        for k in range(KD):
                            mm = pe.matmul(bank(1)[:, s * EX:(s + 1) * EX], xnT[:, s % 2, k, :], rwT[:, k, :],
                                           start=(k == 0 and s == 0), stop=(k == KD - 1), skip_group_check=True)
                        mm.then_inc(lg_ps, 1)

            either(large, aggregate2)

            pe.wait_ge(mem_made, 1)
            mem = mem_b[:, :, :].rearrange("p t e -> p (t e)")
            pe.matmul(bank(2)[:, 0:NT * EX], below[:, :], mem, start=True, stop=False, skip_group_check=True)
            for s in range(1, NT):
                mm = pe.matmul(bank(2)[:, s * EX:NT * EX], ones_b[:, :], mem[:, 0:(NT - s) * EX],
                               start=False, stop=(s == NT - 1), skip_group_check=True)
            for t in range(NT):
                mm = pe.matmul(bank(5)[:, 0:EX], ones_b[:, :], mem_b[:, t, :], start=(t == 0),
                               stop=(t == NT - 1))
            mm.then_inc(rank_ps, 1)
            pe.wait_ge(fc2b_split, 1)
            pe.wait_ge(cw_made, 1)

            def biases(a, b):
                for t in range(a, b + 2):
                    if t < b:
                        if t >= 2:
                            pe.wait_ge(cwT_made, t - 1)
                        pe.transpose(bank(6 + t % 2)[0:3 * EX, 0:P],
                                     cw3[:, t, :, :].rearrange("p i e -> p (i e)"), ident[:, :])\
                          .then_inc(cwT_ps, 1)
                    if t >= a + 2:
                        q = t - 2
                        pe.wait_ge(cwT_made, q + 1)
                        if q >= 3:
                            pe.wait_ge(agg2_out, NT + q - 2)
                        pe.matmul(bank(BIAS_BANKS[q % 3]), cwT[:, q, :], fc2b_3[:, :], start=True, stop=True)\
                          .then_inc(eb_ps, 1)

            biases(0, 3)
            for k in range(TOP):
                pe.wait_ge(spots_made, k + 1)
                for t in range(NT):
                    mm = pe.matmul(bank(1)[:, 0:2 * GT], at_place[:, k, t, :],
                                   in_tile[:, k, t, 1:3, :].rearrange("p q g -> p (q g)"),
                                   start=(k == 0 and t == 0), stop=(k == TOP - 1 and t == NT - 1))
            mm.then_inc(table_ps, 1)
            biases(3, NT)

        @block.scalar
        def _(act):
            def root(n, to, of):
                act.wait_ge(var_made, n)
                act.activation(to, of, ACT.Sqrt).then_inc(root_made, 1)

            root(1, sd[:, 0:3], mv[:, 0:3, 1])
            for t in range(NT + 1):
                if t in (1, 4, 7):
                    g = (t + 2) // 3
                    root(g + 1, sd[:, 3 * g:min(3 * g + 3, NT)], mv[:, 3 * g:min(3 * g + 3, NT), 1])
                if t < NT:
                    act.wait_ge(xnT_ps, t + 1)
                    if t >= 2:
                        act.wait_ge(h_ps, t - 1)
                    act.activation(xnT[:, t % 2, :, :].rearrange("p k n -> p (k n)"), bank(6 + t % 2),
                                   ACT.Copy).then_inc(xnT_made, 1)
                if t >= 1:
                    act.wait_ge(h_ps, t)
                    act.activation(h[:, t - 1, :], bank(4 + (t - 1) % 2), ACT.Copy).then_inc(h_made, 1)

            def ct_block(b):
                for q in range(3):
                    n = 3 * b + q
                    m = min(4, NT - 4 * q)
                    act.wait_ge(ct_ps, n + 1)
                    if n >= 2:
                        act.wait_ge(ctlo_made, n - 1)
                    act.activation(xn[:, n % 2, 0:m * P], bank(6 + n % 2)[:, 0:m * P], ACT.Copy)\
                       .then_inc(ct_copied, 1)
                    act.activation(CT[:, 4 * q:4 * q + m, b * P:(b + 1) * P],
                                   bank(6 + n % 2)[:, 0:m * P].rearrange("p (k n) -> p k n", k=m),
                                   ACT.Copy).then_inc(ct_made, 1)

            for b in range(NT):
                act.wait_ge(counts_ps, b + 1)
                if b >= 1:
                    ct_needed = 3 * b
                    act.wait_ge(ct_ps, ct_needed)
                act.activation(deg[:, b:b + 1], flat[:, 1536 * (b % 2) + NP:1536 * (b % 2) + NP + 1], ACT.Copy)
                act.activation(Cs[:, :], flat[:, 1536 * (b % 2):1536 * (b % 2) + NP], ACT.Copy)\
                   .then_inc(counts_out, 1)
                if b == NT - 1:
                    root(5, sd[:, :], t4[:, 3, :])
                ct_block(b)

            act.wait_ge(dis_made, 1)
            for t in range(NT):
                act.activation(hhi[:, t, :], h[:, t, :], ACT.Copy, scale=dis[:, t:t + 1]).then_inc(hhi_made, 1)
            act.wait_ge(disbc_ps, NT)
            act.activation(dis_bc[:, :], flat[:, 0:NP], ACT.Copy).then_inc(disbc_made, 1)
            act.wait_ge(w2_in, 16)
            act.wait_ge(ctlo_made, 3 * NT)
            act.activation(Whi[:, :, :].rearrange("p k n -> p (k n)"), Wg[:, :, :].rearrange("p k n -> p (k n)"),
                           ACT.Copy).then_inc(w2hi_made, 1)
            act.wait_ge(consts_in, 64)
            act.wait_ge(hlo_made, NT)
            n = 0
            for lo, hi in GROUPS:
                for j in range(KD):
                    act.wait_ge(agg1_scaled, n + 1)
                    act.activation(h1hi[:, j, lo:hi], h1T[:, j, lo:hi], ACT.Relu, bias=b1c[:, j:j + 1])\
                       .then_inc(h1hi_made, 1)
                    act.wait_ge(h1hi_made, n + 1)
                    act.activation(h1T[:, j, lo:hi], h1T[:, j, lo:hi], ACT.Relu, bias=b1c[:, j:j + 1])\
                       .then_inc(h1T_made, 1)
                    n += 1
            for m in range(NT):
                act.wait_ge(h_ps, NT + m + 1)
                if m == 0:
                    act.wait_ge(agg1_ps, 3 * KD)
                act.activation(hhi[:, m, :], bank(5 + m % 2), ACT.Copy, scale=dis[:, m:m + 1])\
                   .then_inc(hhi_made, 1)
            for m in range(NT):
                root(6 + m, sd[:, m:m + 1], mv[:, m, 1:2])
                act.wait_ge(xnT_ps, NT + m + 1)
                if m >= 2:
                    act.wait_ge(lg_ps, m - 1)
                act.activation(xnT[:, m % 2, :, :].rearrange("p k n -> p (k n)"), bank(6 + m % 2),
                               ACT.Copy).then_inc(xnT_made, 1)
            act.wait_ge(var_made, 6 + NT)
            act.activation(mx[:, 3, :], mx[:, 2, :], ACT.Exp).then_inc(root_made, 1)
            for t in range(NT):
                act.wait_ge(cwT_ps, t + 1)
                act.activation(cwT[:, t, :], bank(6 + t % 2)[0:3 * EX, 0:P], ACT.Copy)\
                   .then_inc(cwT_made, 1)

        @block.vector
        def _(v):
            done = 0

            def link(ins):
                nonlocal done
                done += 1
                ins.then_inc(dve, 1)
                v.wait_ge(dve, done)

            v.wait_ge(edges_in, 32)
            link(v.tensor_scalar(src_f[:, :], src_i[:, :], 1.0, None, ALU.add))
            link(v.tensor_scalar(src_i[:, :], dst_i[:, :], P - 1, None, ALU.bitwise_and))
            v.tensor_scalar(dst_f[:, :], src_i[:, :], 1.0, None, ALU.add)
            link(v.tensor_scalar(dst_i[:, :], dst_i[:, :], P.bit_length() - 1, None, ALU.arith_shift_right))
            link(v.tensor_scalar(blk_f[:, :], dst_i[:, :], 0.0, None, ALU.add))
            for b in range(NT):
                f = v.tensor_scalar(flags[:, b * ET:(b + 1) * ET], blk_f[:, :], float(b), None, ALU.is_equal)
            f.then_inc(flags_made, 1)

            def rsqrt(y, s, var, a, b):
                link(v.reciprocal(y, s))
                link(v.tensor_tensor(a, y, y, ALU.mult))
                link(v.tensor_tensor(b, a, var, ALU.mult))
                link(v.tensor_scalar(a, b, -0.5, 1.5, ALU.mult, ALU.add))
                link(v.tensor_tensor(y, y, a, ALU.mult))

            def stats(t):
                link(v.bn_stats(stat[:, :], xres[:, t, :]))
                link(v.bn_aggr(mv[:, t, :], stat[:, :]))

            def hot_d_part(i):
                a, b = ET * i // len(PARTS_AT), ET * (i + 1) // len(PARTS_AT)
                v.tensor_tensor(hot_d[:, a:b, :], iota[:, 0:P].unsqueeze(1).to_broadcast([P, b - a, P]),
                                dst_f[:, a:b].unsqueeze(2).to_broadcast([P, b - a, P]), ALU.is_equal)\
                 .then_inc(hot_d_made, 1)

            at = 2 * GE
            used, weighed = (spare[0:1, at + q * NT * GE:at + (q + 1) * NT * GE].rearrange(
                "p (b i) -> p b i", b=NT) for q in range(2))
            lim = spare[0:1, at + 2 * NT * GE:at + 2 * NT * GE + 3 * NT].rearrange("p (q b) -> p q b", b=NT)

            def groups_used():
                v.wait_ge(flags_summed, 1)
                v.wait_ge(pool_made, 9)
                link(v.tensor_reduce(used, flat[0:1, 0:NT * ET].rearrange("p (b i j) -> p b i j", j=EG, b=NT),
                                     AX.X, ALU.max))

            def ranges():
                for q in range(2):
                    weight = spare[0:1, q * GE:(q + 1) * GE].unsqueeze(1).to_broadcast([1, NT, GE])
                    link(v.scalar_tensor_tensor(weighed, used, 1.0, weight, ALU.min, ALU.mult))
                    link(v.tensor_reduce(lim[:, q, :], weighed, AX.X, ALU.max))
                link(v.tensor_scalar(lim[:, 0, :], lim[:, 0, :], 1.0, None, ALU.max))
                link(v.tensor_scalar(lim[:, 1, :], lim[:, 1, :], -1.0, float(GE), ALU.mult, ALU.add))
                link(v.tensor_scalar(lim[:, 2, :], lim[:, 0, :], -1.0, None, ALU.add))
                link(v.tensor_tensor(lim[:, 1, :], lim[:, 1, :], lim[:, 2, :], ALU.min))
                v.tensor_scalar(rng_i[0:1, 0, :], lim[:, 1, :], 0.0, None, ALU.add)
                v.tensor_scalar(rng_i[0:1, 1, :], lim[:, 0, :], 0.0, None, ALU.add).then_inc(ranges_made, 1)
                v.wait_ge(ranges_made, 1)

            for g in range(4):
                a, b = 3 * g, min(3 * g + 3, NT)
                v.wait_ge(x_in[g], 16)
                if g == 3:
                    v.wait_ge(pool_made, 1)
                for t in range(a, b):
                    stats(t)
                v.tensor_scalar(mv[:, a:b, 1], mv[:, a:b, 1], EPS, None, ALU.add).then_inc(var_made, 1)
                v.wait_ge(root_made, g + 1)
                rsqrt(rs[:, a:b], sd[:, a:b], mv[:, a:b, 1], t4[:, 0, a:b], t4[:, 1, a:b])
                for t in range(a, b):
                    if t >= 2:
                        v.wait_ge(xnT_ps, t - 1)
                    v.tensor_scalar(xn[:, t % 2, :], xres[:, t, :], mv[:, t, 0:1], rs[:, t:t + 1],
                                    ALU.subtract, ALU.mult).then_inc(xn_made, 1)
                    if t in PARTS_AT:
                        v.wait_ge(pool_made, 7)
                        hot_d_part(PARTS_AT.index(t))
                    elif t == 0:
                        groups_used()
            ranges()

            n_hot = v.alloc_register("v_hot")
            v.reg_mov(n_hot, 0)
            for b in range(NT):
                if b >= 1:
                    v.wait_ge(hot_made, n_hot)
                link(v.scalar_tensor_tensor(src_m[:, :], blk_f[:, :], float(b), src_f[:, :],
                                            ALU.is_equal, ALU.mult))
                first = v.value_load(rng_i[0:1, 0, b:b + 1], min_val=0, max_val=GE - 1)
                last = v.value_load(rng_i[0:1, 1, b:b + 1], min_val=1, max_val=GE)
                with v.Fori(first, last) as i:
                    for j in range(EG):
                        v.reg_add(n_hot, n_hot, 1)
                        v.wait_ge(hot_free, n_hot)
                        v.tensor_scalar(hot_s[:, j, :], iota[:, :],
                                        src_m[:, bass.ds(EG * i + j, 1)], None, ALU.is_equal)\
                         .then_inc(hot_made, 1)

            v.wait_ge(counts_out, NT)
            v.tensor_scalar(t4[:, 3, :], deg[:, :], 1.0, None, ALU.add).then_inc(var_made, 1)
            v.wait_ge(var_made, 5)
            v.wait_ge(root_made, 5)
            rsqrt(dis[:, :], sd[:, :], t4[:, 3, :], t4[:, 0, :], t4[:, 1, :])
            link(v.tensor_reduce(many[:, :], deg[:, :], AX.X, ALU.max))
            v.tensor_scalar(many_b[:, :], many[:, :], 4000.0, None, ALU.is_gt).then_inc(dis_made, 1)
            v.wait_ge(many_summed, 1)
            v.tensor_scalar(many_i[0:1, :], bank(5)[0:1, 0:1], 1.0, None, ALU.min).then_inc(many_found, 1)
            v.wait_ge(many_found, 1)
            large = v.value_load(many_i[0:1, 0:1], min_val=0, max_val=1)
            with v.If(large != 0):
                v.wait_ge(ctlo_made, 3 * NT)
                for k in range(NT):
                    v.tensor_tensor(CTx[:, k, :], CT[:, k, :], CTlo[:, k, :], ALU.add).then_inc(whole_made, 1)
            with v.Else():
                v.sem_inc(whole_made, NT)
            v.wait_ge(h_made, NT)
            for t in range(NT):
                v.wait_ge(hhi_made, t + 1)
                v.scalar_tensor_tensor(hlo[:, t, :], h[:, t, :], dis[:, t:t + 1], hhi[:, t, :],
                                       ALU.mult, ALU.subtract).then_inc(hlo_made, 1)
            for t in range(NT):
                if t >= 8:
                    v.wait_ge(disbc_ps, t - 7)
                v.tensor_scalar(diag[:, t % 8, :], ident[:, :], dis[:, t:t + 1], None, ALU.mult)\
                 .then_inc(diag_made, 1)
            v.wait_ge(disbc_made, 1)
            v.wait_ge(zero_out, 32)
            pieces = [(j, lo, hi) for lo, hi in GROUPS for j in range(KD)]
            for n in range(len(pieces) + 1):
                if n < len(pieces):
                    j, lo, hi = pieces[n]
                    v.wait_ge(agg1_ps, n + 1)
                    v.tensor_tensor(h1T[:, j, lo:hi], bank(3 + n % 2)[:, 0:hi - lo], dis_bc[:, lo:hi], ALU.mult)\
                     .then_inc(agg1_scaled, 1)
                if n == 1:
                    v.wait_ge(w2hi_made, 1)
                    v.tensor_tensor(Wlo[:, :, :], Wg[:, :, :], Whi[:, :, :], ALU.subtract).then_inc(w2lo_made, 1)
                if n >= 1:
                    j, lo, hi = pieces[n - 1]
                    v.wait_ge(h1T_made, n)
                    v.tensor_tensor(h1lo[:, j, lo:hi], h1T[:, j, lo:hi], h1hi[:, j, lo:hi], ALU.subtract)\
                     .then_inc(h1lo_made, 1)
            for m in range(NT):
                v.wait_ge(h_ps, NT + m + 1)
                v.wait_ge(hhi_made, NT + m + 1)
                v.scalar_tensor_tensor(hlo[:, m, :], bank(5 + m % 2), dis[:, m:m + 1], hhi[:, m, :],
                                       ALU.mult, ALU.subtract).then_inc(hlo_made, 1)
            def split_fc2b():
                v.wait_ge(fc2b_in, 48)
                v.wait_ge(pool_made, 19)
                limit = float(N + 1 + 2 * EX)
                v.tensor_scalar(in_hi[:, 0:1], pad_row[:, :], limit, None, ALU.is_lt)
                v.tensor_scalar(in_hi[:, 1:2], pad_row[:, :], limit, None, ALU.is_ge)
                link(v.tensor_scalar(fc2b_hi[:, :], fc2b_sb[:, :], 0.0, None, ALU.add))
                link(v.tensor_tensor(fc2b_lo[:, :], fc2b_sb[:, :], fc2b_hi[:, :], ALU.subtract))
                link(v.tensor_scalar(fc2b_lo[:, :], fc2b_lo[:, :], in_hi[0:3 * EX, 1:2], None, ALU.mult))
                v.scalar_tensor_tensor(fc2b_3[:, :], fc2b_hi[:, :], in_hi[0:3 * EX, 0:1], fc2b_lo[:, :],
                                       ALU.mult, ALU.add).then_inc(fc2b_split, 1)

            v.wait_ge(consts_in, 64)
            for t in range(NT):
                f = v.tensor_tensor(xres[:, t, :], xres[:, t, :], b2_bc[:, :], ALU.add)
            link(f)
            v.wait_ge(h_ps, 2 * NT)
            for m in range(NT):
                v.wait_ge(agg2_ps, m + 1)
                f = v.scalar_tensor_tensor(xres[:, m, :], bank(3 + m % 2), dis[:, m:m + 1], xres[:, m, :],
                                           ALU.mult, ALU.add)
                f.then_inc(agg2_out, 1)
                v.wait_ge(agg2_out, m + 1)
                stats(m)
                v.tensor_scalar(mv[:, m, 1:2], mv[:, m, 1:2], EPS, None, ALU.add).then_inc(var_made, 1)
                v.wait_ge(var_made, 6 + m)
                v.wait_ge(root_made, 6 + m)
                rsqrt(rs[:, m:m + 1], sd[:, m:m + 1], mv[:, m, 1:2], t4[:, 0, m:m + 1], t4[:, 1, m:m + 1])
                v.tensor_scalar(xn1[:, m, :], xres[:, m, :], mv[:, m, 0:1], rs[:, m:m + 1],
                                ALU.subtract, ALU.mult).then_inc(xn_made, 1)
                if m == 4:
                    split_fc2b()

            def add_biases(a, b):
                for t in range(a, b):
                    v.wait_ge(eb_ps, t + 1)
                    v.tensor_tensor(xres[:, t, :], xres[:, t, :], bank(BIAS_BANKS[t % 3]), ALU.add)\
                     .then_inc(agg2_out, 1)

            v.wait_ge(lg_ps, NT)
            v.wait_ge(pool_made, 19)
            bc = lambda a: a.unsqueeze(2).to_broadcast([P, NT, EX])
            link(v.tensor_tensor(lg[:, :, :], bank(1)[:, 0:NT * EX].rearrange("p (t e) -> p t e", t=NT),
                                 rb_bc[:, :].unsqueeze(1).to_broadcast([P, NT, EX]), ALU.add))
            for k in range(TOP):
                link(v.tensor_reduce(mx[:, k, :], lg[:, :, :], AX.X, ALU.max))
                link(v.tensor_tensor(sc8[:, 0, :, :], lg[:, :, :], bc(mx[:, k, :]), ALU.is_equal))
                link(v.tensor_tensor(sc8[:, 1, :, :], sc8[:, 0, :, :], iota_e[:, :, :], ALU.mult))
                link(v.tensor_reduce(mx[:, 4, :], sc8[:, 1, :, :], AX.X, ALU.min))
                link(v.tensor_tensor(top[:, k, :, :], iota_e[:, :, :], bc(mx[:, 4, :]), ALU.is_equal))
                if k == 0:
                    link(v.scalar_tensor_tensor(lg[:, :, :], top[:, 0, :, :], -3.0e38, lg[:, :, :],
                                                ALU.mult, ALU.add))
            v.tensor_tensor(mx[:, 2, :], mx[:, 1, :], mx[:, 0, :], ALU.subtract).then_inc(var_made, 1)
            link(v.tensor_tensor(sc8[:, 0, :, :], top[:, 0, :, :], top[:, 1, :, :], ALU.add))
            v.tensor_tensor(mem_b[:, :, :], sc8[:, 0, :, :], bc(valid[:, :]), ALU.mult).then_inc(mem_made, 1)
            v.wait_ge(var_made, 6 + NT)
            v.wait_ge(root_made, 6 + NT)
            link(v.tensor_scalar(mx[:, 4, :], mx[:, 3, :], 1.0, None, ALU.add))
            link(v.reciprocal(wts[:, 0, :], mx[:, 4, :]))
            link(v.tensor_tensor(wts[:, 1, :], wts[:, 0, :], mx[:, 3, :], ALU.mult))
            link(v.tensor_tensor(sc8[:, 0, :, :], top[:, 0, :, :], bc(wts[:, 0, :]), ALU.mult))
            link(v.tensor_tensor(sc8[:, 1, :, :], top[:, 1, :, :], bc(wts[:, 1, :]), ALU.mult))
            link(v.tensor_tensor(cw[:, :, :], sc8[:, 0, :, :], sc8[:, 1, :, :], ALU.add))
            link(v.tensor_scalar(cw3[:, :, 0, :].bitcast(F32R), cw[:, :, :], 0.0, None, ALU.add))
            v.tensor_tensor(cw3[:, :, 1, :], cw[:, :, :], cw3[:, :, 0, :], ALU.subtract)
            v.tensor_scalar(cw3[:, :, 2, :], cw3[:, :, 0, :], 0.0, None, ALU.add).then_inc(cw_made, 1)
            for q in (wts[:, 0, :], wts[:, 1, :], token[:, :]):
                f = v.tensor_tensor(q, q, valid[:, :], ALU.mult)
            link(f)
            v.wait_ge(rank_ps, 1)
            link(v.tensor_scalar(e8[:, 0, :], bank(5)[:, 0:EX], 1.0, None, ALU.max))
            link(v.tensor_tensor(cmp8[:, :, :], e8[:, 0, :].unsqueeze(2).to_broadcast([P, EX, NT]),
                                 thr[:, :, :], ALU.is_gt))
            link(v.tensor_reduce(e8[:, 1, :], cmp8[:, :, :], AX.X, ALU.add))
            a, b = 1, 2
            for s in (1, 2, 4):
                v.tensor_scalar(e8[:, b, 0:s], e8[:, a, 0:s], 0.0, None, ALU.add)
                link(v.tensor_tensor(e8[:, b, s:EX], e8[:, a, s:EX], e8[:, a, 0:EX - s], ALU.add))
                a, b = b, b + 1
            link(v.tensor_tensor(e8[:, 5, :], e8[:, 4, :], e8[:, 1, :], ALU.subtract))
            v.tensor_scalar(gstart[0:1, 0:EX], e8[0:1, 5, :], 0.0, None, ALU.add)
            v.tensor_scalar(gstart[0:1, EX:EX + 1], e8[0:1, 4, EX - 1:EX], 0.0, None, ALU.add)
            link(v.tensor_scalar(e8[:, 2, :], e8[:, 5, :], float(P), None, ALU.mult))
            link(v.tensor_tensor(rank[:, :, :], bank(2)[:, 0:NT * EX].rearrange("p (t e) -> p t e", t=NT),
                                 e8[:, 2, :].unsqueeze(1).to_broadcast([P, NT, EX]), ALU.add))
            for k in range(TOP):
                link(v.tensor_tensor(sc8[:, 0, :, :], top[:, k, :, :], rank[:, :, :], ALU.mult))
                link(v.tensor_reduce(mx[:, 4, :], sc8[:, 0, :, :], AX.X, ALU.add))
                link(v.tensor_scalar(slot[:, k, :], mx[:, 4, :], 0.0, None, ALU.add))
            v.tensor_scalar(part_i[:, 0, :, :], slot[:, :, :], P.bit_length() - 1, None, ALU.arith_shift_right)
            link(v.tensor_scalar(part_i[:, 1, :, :], slot[:, :, :], P - 1, None, ALU.bitwise_and))
            v.tensor_scalar(part_f[:, 0, :, :], part_i[:, 0, :, :], 0.0, None, ALU.add)
            link(v.tensor_scalar(part_f[:, 1, :, :], part_i[:, 1, :, :], 1.0, None, ALU.add))
            for k in range(TOP):
                over = lambda a, n: a.unsqueeze(2).to_broadcast([P, NT, n])
                v.tensor_tensor(at_place[:, k, :, :], iota_p[:, :].unsqueeze(1).to_broadcast([P, NT, P]),
                                over(part_f[:, 1, k, :], P), ALU.is_equal)
                link(v.tensor_tensor(in_tile[:, k, :, 0, :], iota_g[:, :, :], over(part_f[:, 0, k, :], GT),
                                     ALU.is_equal))
                v.tensor_tensor(in_tile[:, k, :, 1, :], in_tile[:, k, :, 0, :], over(token[:, :], GT), ALU.mult)
                v.tensor_tensor(in_tile[:, k, :, 2, :], in_tile[:, k, :, 0, :], over(wts[:, k, :], GT),
                                ALU.mult).then_inc(spots_made, 1)
            add_biases(0, 3)
            v.wait_ge(table_ps, 1)
            v.tensor_copy(tok_w[:, :], bank(1)[:, GT:2 * GT])
            link(v.tensor_copy(id_w[:, 0, :], bank(1)[:, 0:GT]))
            link(v.tensor_scalar(id_w[:, 1, :], id_w[:, 0, :], 0.0, pad_row[:, :], ALU.is_equal, ALU.mult))
            link(v.scalar_tensor_tensor(tok_i[:, :], id_w[:, 0, :], -1.0, id_w[:, 1, :], ALU.add, ALU.add))
            v.tensor_scalar(next_i[:, :], tok_i[:, 0:1], 0.0, None, ALU.add).then_inc(next_set, 1)
            add_biases(3, NT)


def expert_block(nc, outer, env):
    wall, fc1b, out = env["wall"], env["fc1b"], env["out"]
    ident, raw, tok_i, tok_w, xg, next_i, gstart, ps = (env[k] for k in (
        "ident", "raw", "tok_i", "tok_w", "xg", "next_i", "gstart", "ps"))
    raw_in, next_set, x_loaded, out_stored, rows_dram = (env[k] for k in (
        "raw_in", "next_set", "x_loaded", "out_stored", "rows_dram"))

    with ExitStack() as ctx:
        def sb(name, shape, dt):
            return ctx.enter_context(nc.sbuf_tensor(name, shape, dt))

        def sem(name):
            return ctx.enter_context(nc.semaphore(name))

        sb("raw_place2", [P, CH, CW], F32)
        whi = sb("whi", [P, CH, KD, D], F32R)
        wlo = sb("wlo", [P, CH, KD, D], F32R)
        bias = sb("bias", [P, 2, 2, D], F32)
        row_w = sb("row_w", [P, 1], F32)
        row_i = sb("row_i", [P, 1], I32)
        xhi = sb("xhi", [P, KD, P], F32R)
        xlo = sb("xlo", [P, KD, P], F32R)
        t1 = sb("t1", [P, 2, D], F32)
        sl = sb("sl", [P, 2, D], F32)
        a = sb("a", [P, 2, D], F32)
        ahi = sb("ahi", [P, 2, KD, P], F32R)
        alo = sb("alo", [P, 2, KD, P], F32R)
        ysb = sb("ysb", [P, D], F32)

        bias_in = sem("bias_in")
        bias_free = sem("bias_free")
        hi_dve = sem("hi_dve")
        hi_act = sem("hi_act")
        lo_dve = sem("lo_dve")
        lo_pool = sem("lo_pool")
        xT_ps = sem("xT_ps")
        xhi_made = sem("xhi_made")
        xlo_made = sem("xlo_made")
        fc1_ps = sem("fc1_ps")
        t1_made = sem("t1_made")
        sl_made = sem("sl_made")
        u_made = sem("u_made")
        a_made = sem("a_made")
        aT_ps = sem("aT_ps")
        ahi_made = sem("ahi_made")
        alo_made = sem("alo_made")
        y_ps = sem("y_ps")
        y_out = sem("y_out")
        y_added = sem("y_added")
        rows_set = sem("rows_set")
        tick = sem("tick")

        XT, Y = 6, 7
        bank = lambda i: ps[:, i, :]
        chunk = lambda w, c: w[:, c, :, :].rearrange("p k n -> p (k n)")

        def hi_ready(eng, e, c):
            if c < 2:
                eng.wait_ge(hi_dve, 2 * e + c + 1)
            else:
                eng.wait_ge(hi_act, (CH - 2) * e + ACT_CHUNKS.index(c) + 1)

        def lo_ready(eng, e, c):
            if c < 3:
                eng.wait_ge(lo_dve, 3 * e + c + 1)
            else:
                eng.wait_ge(lo_pool, 3 * e + c - 2)

        def tiles(eng, e):
            first = eng.value_load(gstart[0:1, bass.ds(e, 1)], min_val=0, max_val=MAXT - 1)
            last = eng.value_load(gstart[0:1, bass.ds(e + 1, 1)], min_val=1, max_val=MAXT)
            return first, last

        block = ctx.enter_context(nc.Block())

        @block.sync
        def _(sp):
            def load_bias(e):
                sp.dma_start(bias[:, :, :, :].rearrange("p q g n -> p (q g n)"),
                             fc1b[bass.ds(e, 1), :].rearrange("a n -> (a n)").partition_broadcast(P))\
                  .then_inc(bias_in, 16)

            load_bias(0)
            with sp.Fori(0, EX - 1) as e:
                for c in range(CH):
                    hi_ready(sp, e, c)
                    sp.sem_inc(tick, 1)
                    lo_ready(sp, e, c)
                    sp.sem_inc(tick, 1)
                    sp.dma_start(raw[:, c, :], wall[bass.ds(e * CH + CH + c, 1), :, :]
                                 .rearrange("a p n -> (a p) n")).then_inc(raw_in[c], 16)
                sp.wait_ge(bias_free, e + 1)
                load_bias(e + 1)

        @block.gpsimd
        def _(pool):
            def add_y():
                pool.indirect_dma_start(out, bass.IndirectOffsetOnAxis(row_i[:, :], 0), ysb[:, :], None,
                                        compute_op=ALU.add).then_inc(y_added, 16)

            def load_x(n):
                pool.wait_ge(next_set, n)
                pool.sem_inc(tick, 1)
                pool.indirect_dma_start(xg[:, :], None, rows_dram,
                                        bass.IndirectOffsetOnAxis(next_i[:, :], 0)).then_inc(x_loaded, 16)

            pool.iota(row_i[:, :], pattern=[[0, 1]], base=N, channel_multiplier=1)
            pool.memset(row_w[:, :], 0.0).then_inc(rows_set, 1)
            pool.wait_ge(rows_set, 1)
            pool.dma_start(ysb[0:1, :], rows_dram[0:1, 0:D]).then_inc(y_added, 16)
            pool.wait_ge(out_stored, 16 * NT)
            pool.wait_ge(xT_ps, 1)
            load_x(2)
            with pool.Fori(0, EX) as e:
                for c in (3, 4, 5):
                    hi_ready(pool, e, c)
                    pool.tensor_tensor(chunk(wlo, c), raw[:, c, :], chunk(whi, c), ALU.subtract)\
                        .then_inc(lo_pool, 1)
                first, last = tiles(pool, e)
                with pool.Fori(first, last) as g:
                    pool.wait_ge(y_out, g + 1)
                    pool.wait_ge(y_added, 16 * g + 16)
                    pool.sem_inc(tick, 1)
                    add_y()
                    pool.wait_ge(xT_ps, g + 2)
                    pool.sem_inc(tick, 1)
                    load_x(g + 3)
            total = pool.value_load(gstart[0:1, EX:EX + 1], min_val=1, max_val=MAXT)
            pool.wait_ge(y_out, total + 1)
            pool.wait_ge(y_added, 16 * total + 16)
            pool.sem_inc(tick, 1)
            add_y()
            pool.wait_ge(y_added, 16 * total + 32)
            pool.sem_inc(tick, 1)

        @block.tensor
        def _(pe):
            def transposes(to, of):
                for k in range(KD):
                    tr = pe.transpose(to[:, k * P:(k + 1) * P], of[:, k * P:(k + 1) * P], ident[:, :])
                return tr

            pe.wait_ge(x_loaded, 16)
            transposes(bank(Y), xg).then_inc(y_ps, 1)
            transposes(bank(XT), xg).then_inc(xT_ps, 1)
            pe.sem_inc(fc1_ps, 1)

            def product(o, hi, lo, c, e=None, part=(0, 3 * KD), start=True, stop=True):
                steps = [(k, l, w) for l, w in ((hi, whi), (lo, whi), (hi, wlo)) for k in range(KD)]
                for n in range(*part):
                    if n == 0:
                        hi_ready(pe, e, c)
                    if n == 2 * KD:
                        lo_ready(pe, e, c)
                    k, l, w = steps[n]
                    mm = pe.matmul(o, l[:, k, :], w[:, c, k, :], start=start and n == 0,
                                   stop=stop and n == len(steps) - 1)
                return mm

            with pe.Fori(0, EX) as e:
                first, last = tiles(pe, e)
                with pe.Fori(first, last) as g:
                    def turn(q):
                        pe.wait_ge(a_made, 2 * g + q + 1)
                        transposes(bank(4 + q), a[:, q, :]).then_inc(aT_ps, 1)

                    pe.wait_ge(xhi_made, g + 1)
                    product(bank(0), xhi, xlo, 0, e, (0, KD), stop=False)
                    pe.wait_ge(xlo_made, g + 1)
                    product(bank(0), xhi, xlo, 0, e, (KD, 3 * KD)).then_inc(fc1_ps, 1)
                    for c in (1, 2):
                        product(bank(c), xhi, xlo, c, e).then_inc(fc1_ps, 1)
                    product(bank(3), xhi, xlo, 3, e, (0, KD), stop=False)
                    turn(0)
                    product(bank(3), xhi, xlo, 3, e, (KD, 3 * KD)).then_inc(fc1_ps, 1)
                    pe.wait_ge(ahi_made, 2 * g + 1)
                    pe.wait_ge(alo_made, 2 * g + 1)
                    pe.wait_ge(y_out, g + 1)
                    product(bank(Y), ahi[:, 0, :, :], alo[:, 0, :, :], 4, e, (0, 7), stop=False)
                    turn(1)
                    product(bank(Y), ahi[:, 0, :, :], alo[:, 0, :, :], 4, e, (7, 3 * KD), stop=False)
                    pe.wait_ge(x_loaded, 16 * g + 32)
                    transposes(bank(XT), xg).then_inc(xT_ps, 1)
                    pe.wait_ge(ahi_made, 2 * g + 2)
                    product(bank(Y), ahi[:, 1, :, :], alo[:, 1, :, :], 5, e, (0, KD), start=False, stop=False)
                    pe.wait_ge(alo_made, 2 * g + 2)
                    product(bank(Y), ahi[:, 1, :, :], alo[:, 1, :, :], 5, e, (KD, 3 * KD), start=False)\
                        .then_inc(y_ps, 1)

        @block.scalar
        def _(act):
            def weigh_y(g):
                act.wait_ge(y_added, 16 * g + 16)
                act.wait_ge(rows_set, g + 1)
                act.wait_ge(y_ps, g + 1)
                act.activation(ysb[:, :], bank(Y), ACT.Copy, scale=row_w[:, :]).then_inc(y_out, 1)

            def copy_x(n):
                act.wait_ge(xT_ps, n)
                act.activation(xhi[:, :, :].rearrange("p k n -> p (k n)"), bank(XT), ACT.Copy)\
                   .then_inc(xhi_made, 1)

            act.preload_act_table(ACT.Silu)
            copy_x(1)
            with act.Fori(0, EX) as e:
                for c in ACT_CHUNKS:
                    if c == 4:
                        first, last = tiles(act, e)
                        act.wait_ge(y_ps, first + 1)
                    act.wait_ge(raw_in[c], 16 * e + 16)
                    act.activation(chunk(whi, c), raw[:, c, :], ACT.Copy).then_inc(hi_act, 1)
                with act.Fori(first, last) as g:
                    weigh_y(g)
                    for q in range(2):
                        act.wait_ge(t1_made, 2 * g + q + 1)
                        act.activation(sl[:, q, :], t1[:, q, :], ACT.Silu).then_inc(sl_made, 1)
                        act.wait_ge(aT_ps, 2 * g + q + 1)
                        act.activation(ahi[:, q, :, :].rearrange("p k n -> p (k n)"), bank(4 + q), ACT.Copy)\
                           .then_inc(ahi_made, 1)
                    copy_x(g + 2)
            total = act.value_load(gstart[0:1, EX:EX + 1], min_val=1, max_val=MAXT)
            weigh_y(total)

        @block.vector
        def _(v):
            def lower_x(n):
                v.wait_ge(xhi_made, n)
                v.tensor_tensor(xlo[:, :, :].rearrange("p k n -> p (k n)"), bank(XT),
                                xhi[:, :, :].rearrange("p k n -> p (k n)"), ALU.subtract).then_inc(xlo_made, 1)

            def split_upper(e):
                for c in range(2):
                    v.wait_ge(raw_in[c], 16 * e + 16)
                    v.tensor_copy(chunk(whi, c), raw[:, c, :]).then_inc(hi_dve, 1)

            def set_next(n):
                v.tensor_scalar(next_i[:, :], tok_i[:, bass.ds(n - 1, 1)], 0.0, None, ALU.add)\
                 .then_inc(next_set, 1)

            split_upper(0)
            v.wait_ge(x_loaded, 16)
            set_next(2)
            lower_x(1)
            with v.Fori(0, EX) as e:
                for c in range(3):
                    if c == 2:
                        v.wait_ge(bias_in, 16 * e + 16)
                    hi_ready(v, e, c)
                    v.tensor_tensor(chunk(wlo, c), raw[:, c, :], chunk(whi, c), ALU.subtract).then_inc(lo_dve, 1)
                first, last = tiles(v, e)
                with v.Fori(first, last) as g:
                    def gate(q):
                        v.wait_ge(fc1_ps, 4 * g + 2 * q + 2)
                        v.tensor_tensor(t1[:, q, :], bank(2 * q), bias[:, q, 0, :], ALU.add).then_inc(t1_made, 1)

                    def up(q):
                        v.wait_ge(fc1_ps, 4 * g + 2 * q + 3)
                        v.tensor_tensor(a[:, q, :], bank(2 * q + 1), bias[:, q, 1, :], ALU.add)\
                         .then_inc(u_made, 1)
                        v.wait_ge(u_made, 2 * g + q + 1)
                        v.wait_ge(sl_made, 2 * g + q + 1)
                        v.tensor_tensor(a[:, q, :], a[:, q, :], sl[:, q, :], ALU.mult).then_inc(a_made, 1)

                    def lower_a(q):
                        v.wait_ge(ahi_made, 2 * g + q + 1)
                        v.tensor_tensor(alo[:, q, :, :].rearrange("p k n -> p (k n)"), bank(4 + q),
                                        ahi[:, q, :, :].rearrange("p k n -> p (k n)"), ALU.subtract)\
                         .then_inc(alo_made, 1)

                    gate(0)
                    up(0)
                    gate(1)
                    lower_a(0)
                    up(1)
                    with v.If(g + 1 == last):
                        with v.If(e != EX - 1):
                            split_upper(e + 1)
                    lower_a(1)
                    lower_x(g + 2)
                    v.wait_ge(x_loaded, 16 * g + 32)
                    set_next(g + 3)
                    v.wait_ge(y_added, 16 * g + 32)
                    v.tensor_scalar(row_i[:, :], tok_i[:, bass.ds(g, 1)], 0.0, None, ALU.add)
                    v.tensor_scalar(row_w[:, :], tok_w[:, bass.ds(g, 1)], 0.0, None, ALU.add)\
                     .then_inc(rows_set, 1)
                v.sem_inc(bias_free, 1)


def kernel(**inputs):
    import numpy as np
    import concourse.bacc as bacc
    from concourse.bass_utils import run_bass_kernel_spmd

    arr = {k: np.asarray(v) for k, v in inputs.items()}

    def edges(a, pad):
        whole = np.full(ET * P, pad, np.int32)
        whole[:EDGES] = a
        return np.ascontiguousarray(whole.reshape(ET, P).T)

    fc1 = arr["L0_ffn_fc1_w"].reshape(EX, 2, 2, D, KD, P).transpose(0, 2, 1, 5, 4, 3).reshape(EX, 4, P, CW)
    fc2 = arr["L0_ffn_fc2_w"].reshape(EX, D, 2, KD, P).transpose(0, 2, 4, 3, 1).reshape(EX, 2, P, CW)
    arrays = {
        "x": arr["x"],
        "src": edges(arr["src"], 0),
        "dst": edges(arr["dst"], NO_NODE),
        "W1": arr["L0_gnn_W1"],
        "b1": np.ascontiguousarray(arr["L0_gnn_b1"].reshape(KD, P).T),
        "W2": arr["L0_gnn_W2"],
        "b2": arr["L0_gnn_b2"],
        "rw": np.ascontiguousarray(arr["L0_ffn_router_w"].T),
        "rb": arr["L0_ffn_router_b"],
        "wall": np.ascontiguousarray(np.concatenate([fc1, fc2], axis=1).reshape(EX * CH, P, CW)),
        "fc1b": np.ascontiguousarray(
            arr["L0_ffn_fc1_b"].reshape(EX, 2, 2, D).transpose(0, 2, 1, 3).reshape(EX, 4 * D)),
        "fc2b": arr["L0_ffn_fc2_b"],
    }
    nc = bacc.Bacc("TRN2", target_bir_lowering=False, num_devices=1)
    args = [nc.dram_tensor(f"in_{k}", a.shape, mybir.dt.from_np(a.dtype), kind="ExternalInput").ap()
            for k, a in arrays.items()]
    out = nc.dram_tensor("out", (N + P, D), F32, kind="ExternalOutput").ap()
    build(nc, *args, out)
    r = run_bass_kernel_spmd(nc, [{f"in_{k}": a for k, a in arrays.items()}], core_ids=[0])
    return r.results[0]["out"][:N]
```
